# Optimizing a Trainium2 kernel written in Bass

```python
import numpy as np
import jax
import jax.numpy as jnp

def _softmax(x, axis=-1):
    return jax.nn.softmax(x, axis=axis)

def _gelu(x):
    return jax.nn.gelu(x, approximate=True)

def _silu(x):
    return jax.nn.silu(x)

def _sigmoid(x):
    return jax.nn.sigmoid(x)

def _layernorm(x, axis=-1, eps=1e-05):
    m = jnp.mean(x, axis=axis, keepdims=True)
    v = jnp.var(x, axis=axis, keepdims=True)
    return (x - m) / jnp.sqrt(v + eps)

def _scatter_add(tgt, idx, src, axis=0):
    return tgt.at[idx].add(src)

def _segment_sum(src, seg, n):
    return jax.ops.segment_sum(src, seg, n)
kernel_name = 'mk_flamingo_gated_d2_seqx_r8_f67ece'

def setup_inputs(seed: int=0):
    np.random.seed(seed)
    _w = jnp.asarray

    def _rec_inputs():
        import jax
        import jax.numpy as jnp
        _rk = jax.random.key(seed)
        x = 7.22e-05 + 1 * jax.random.normal(jax.random.fold_in(_rk, 1), (8, 256, 256), jnp.float32)
        _lenS = 256 - jax.random.randint(jax.random.fold_in(_rk, 7), (8,), 0, max(1, 256 // 4) + 1, jnp.int32)
        _lenS2 = 64 - jax.random.randint(jax.random.fold_in(_rk, 8), (8,), 0, max(1, 64 // 4) + 1, jnp.int32)
        _ctx_2048P = jax.random.normal(jax.random.fold_in(_rk, 11), (8, 16, 256), jnp.float32)
        _ctx_2048c = jax.random.dirichlet(jax.random.fold_in(_rk, 511), 0.3 * jnp.ones((16,), jnp.float32), (8, 64))
        _ctx_2048t = jnp.einsum('bsk,bkd->bsd', _ctx_2048c, _ctx_2048P)
        _ctx_2048t = _ctx_2048t * jax.lax.rsqrt(jnp.mean(jnp.square(_ctx_2048t)) + 1e-12) * 0.953939
        ctx_2048 = -0.000514642 + 1.00011 * (_ctx_2048t + 0.3 * jax.random.normal(jax.random.fold_in(_rk, 611), (8, 64, 256), jnp.float32))
        _g = jax.random.normal(jax.random.fold_in(_rk, 9001), (2, 2), jnp.float32)
        _g = jnp.sign(_g) * jnp.maximum(jnp.abs(_g), 1.0) + (_g == 0) * 1.0
        g_xattn = _g[0]
        g_ffn = _g[1]
        return (x, ctx_2048, g_xattn, g_ffn)
    x, ctx_2048, g_xattn, g_ffn = _rec_inputs()

    def _L0_xattn_setup():
        import jax, jax.numpy as jnp
        import numpy as np
        HIDDEN = 256
        NUM_HEADS = 16
        NUM_KV_HEADS = 4
        HEAD_DIM = 128
        ROPE_THETA = 10000.0
        EPS = 1e-06

        def rms_norm(x, w, eps=EPS):
            var = jnp.mean(jnp.square(x), axis=-1, keepdims=True)
            return x * jax.lax.rsqrt(var + eps) * w

        def rope_cache(L, head_dim, theta, dtype):
            inv_freq = 1.0 / theta ** (jnp.arange(0, head_dim, 2, dtype=jnp.float32) / head_dim)
            t = jnp.arange(L, dtype=jnp.float32)
            freqs = jnp.outer(t, inv_freq)
            emb = jnp.concatenate([freqs, freqs], -1)
            cos = jnp.cos(emb).astype(dtype)[None, :, None, :]
            sin = jnp.sin(emb).astype(dtype)[None, :, None, :]
            return (cos, sin)

        def rotate_half(x):
            x1, x2 = jnp.split(x, 2, axis=-1)
            return jnp.concatenate([-x2, x1], axis=-1)
        key = jax.random.key(seed)
        ks = jax.random.split(key, 10)
        B, L, T = (2, 256, 64)
        q_out = NUM_HEADS * HEAD_DIM
        kv_out = NUM_KV_HEADS * HEAD_DIM
        s = lambda fan_in: 1.0 / np.sqrt(fan_in)
        return {'x': jax.random.normal(ks[0], (B, L, HIDDEN), jnp.float32), 'h_ctx_kv': jax.random.normal(ks[1], (B, T, HIDDEN), jnp.float32), 'wq': jax.random.normal(ks[2], (HIDDEN, q_out), jnp.float32) * s(HIDDEN), 'wk': jax.random.normal(ks[3], (HIDDEN, kv_out), jnp.float32) * s(HIDDEN), 'wv': jax.random.normal(ks[4], (HIDDEN, kv_out), jnp.float32) * s(HIDDEN), 'wo': jax.random.normal(ks[5], (q_out, HIDDEN), jnp.float32) * s(q_out), 'wk_ctx': jax.random.normal(ks[6], (HIDDEN, kv_out), jnp.float32) * s(HIDDEN), 'wv_ctx': jax.random.normal(ks[7], (HIDDEN, kv_out), jnp.float32) * s(HIDDEN), 'q_norm_w': jnp.ones((HEAD_DIM,), jnp.float32), 'k_norm_w': jnp.ones((HEAD_DIM,), jnp.float32)}
    _L0_xattn_all = _L0_xattn_setup()
    _L0_xattn_in = {k: v for k, v in _L0_xattn_all.items() if k in ('wq', 'wk', 'wv', 'wo', 'wk_ctx', 'wv_ctx', 'q_norm_w', 'k_norm_w')}
    del _L0_xattn_all

    def _L0_ffn_setup():
        import jax, jax.numpy as jnp
        import numpy as np
        B, S, D, FF, E = (4, 256, 256, 1024, 2)
        key = jax.random.key(seed)
        k0, k1, k2, k3, k4 = jax.random.split(key, 5)
        s = 0.02
        return {'hidden_states': jax.random.normal(k0, (B, S, D), jnp.float32), 'gate_w': jax.random.normal(k1, (E, D), jnp.float32) * s, 'w_gate': jax.random.normal(k2, (E, FF, D), jnp.float32) * s, 'w_up': jax.random.normal(k3, (E, FF, D), jnp.float32) * s, 'w_down': jax.random.normal(k4, (E, D, FF), jnp.float32) * s}
    _L0_ffn_all = _L0_ffn_setup()
    _L0_ffn_in = {k: v for k, v in _L0_ffn_all.items() if k in ('gate_w', 'w_gate', 'w_up', 'w_down')}
    del _L0_ffn_all

    def _L1_xattn_setup():
        import jax, jax.numpy as jnp
        import numpy as np
        NUM_HEADS = 16

        def _qdq(x):
            s = jnp.maximum(jnp.max(jnp.abs(x), axis=-1, keepdims=True) / 127.0, 1e-08)
            return jnp.clip(jnp.round(x / s), -127.0, 127.0) * s
        key = jax.random.key(seed)
        ks = jax.random.split(key, 8)
        B, N, M, D = (2, 512, 64, 256)
        w_std = 0.02
        return {'x': jax.random.normal(ks[0], (B, N, D), jnp.float32), 'cond': jax.random.normal(ks[1], (B, M, D), jnp.float32), 'wq': jax.random.normal(ks[2], (D, D), jnp.float32) * w_std, 'bq': jax.random.normal(ks[3], (D,), jnp.float32) * w_std, 'wkv': jax.random.normal(ks[4], (2 * D, D), jnp.float32) * w_std, 'bkv': jax.random.normal(ks[5], (2 * D,), jnp.float32) * w_std, 'wp': jax.random.normal(ks[6], (D, D), jnp.float32) * w_std, 'bp': jax.random.normal(ks[7], (D,), jnp.float32) * w_std}
    _L1_xattn_all = _L1_xattn_setup()
    _L1_xattn_in = {k: v for k, v in _L1_xattn_all.items() if k in ('wq', 'bq', 'wkv', 'bkv', 'wp', 'bp')}
    del _L1_xattn_all

    def _L1_ffn_setup():
        import jax, jax.numpy as jnp
        import numpy as np
        H = 256
        I = 128
        K = 8
        E = 128
        TOPK = 4
        EPS = 1e-08
        key = jax.random.key(seed)
        ks = jax.random.split(key, 10)
        s = 0.02
        return {'x': jax.random.normal(ks[0], (4, 256, H), jnp.float32), 'w_router': jax.random.normal(ks[1], (H, E), jnp.float32) * s, 'w_gate': jax.random.normal(ks[2], (H, K * I), jnp.float32) * s, 'w_up': jax.random.normal(ks[3], (H, K * I), jnp.float32) * s, 'w_down': jax.random.normal(ks[4], (I, H), jnp.float32) * s, 'amplitudes': jax.random.normal(ks[5], (E, K, 2), jnp.float32) * 0.1, 'expert_scale': jnp.ones((E,), jnp.float32), 'shared_w_gate': jax.random.normal(ks[6], (H, 2 * I), jnp.float32) * s, 'shared_w_up': jax.random.normal(ks[7], (H, 2 * I), jnp.float32) * s, 'shared_w_down': jax.random.normal(ks[8], (2 * I, H), jnp.float32) * s}
    _L1_ffn_all = _L1_ffn_setup()
    _L1_ffn_in = {k: v for k, v in _L1_ffn_all.items() if k in ('w_router', 'w_gate', 'w_up', 'w_down', 'amplitudes', 'expert_scale', 'shared_w_gate', 'shared_w_up', 'shared_w_down')}
    del _L1_ffn_all
    return {'x': x, 'ctx_2048': ctx_2048, 'g_xattn': g_xattn, 'g_ffn': g_ffn, 'L0_xattn_wq': _L0_xattn_in['wq'], 'L0_xattn_wk': _L0_xattn_in['wk'], 'L0_xattn_wv': _L0_xattn_in['wv'], 'L0_xattn_wo': _L0_xattn_in['wo'], 'L0_xattn_wk_ctx': _L0_xattn_in['wk_ctx'], 'L0_xattn_wv_ctx': _L0_xattn_in['wv_ctx'], 'L0_xattn_q_norm_w': _L0_xattn_in['q_norm_w'], 'L0_xattn_k_norm_w': _L0_xattn_in['k_norm_w'], 'L0_ffn_gate_w': _L0_ffn_in['gate_w'], 'L0_ffn_w_gate': _L0_ffn_in['w_gate'], 'L0_ffn_w_up': _L0_ffn_in['w_up'], 'L0_ffn_w_down': _L0_ffn_in['w_down'], 'L1_xattn_wq': _L1_xattn_in['wq'], 'L1_xattn_bq': _L1_xattn_in['bq'], 'L1_xattn_wkv': _L1_xattn_in['wkv'], 'L1_xattn_bkv': _L1_xattn_in['bkv'], 'L1_xattn_wp': _L1_xattn_in['wp'], 'L1_xattn_bp': _L1_xattn_in['bp'], 'L1_ffn_w_router': _L1_ffn_in['w_router'], 'L1_ffn_w_gate': _L1_ffn_in['w_gate'], 'L1_ffn_w_up': _L1_ffn_in['w_up'], 'L1_ffn_w_down': _L1_ffn_in['w_down'], 'L1_ffn_amplitudes': _L1_ffn_in['amplitudes'], 'L1_ffn_expert_scale': _L1_ffn_in['expert_scale'], 'L1_ffn_shared_w_gate': _L1_ffn_in['shared_w_gate'], 'L1_ffn_shared_w_up': _L1_ffn_in['shared_w_up'], 'L1_ffn_shared_w_down': _L1_ffn_in['shared_w_down']}

def reference(x, ctx_2048, g_xattn, g_ffn, L0_xattn_wq, L0_xattn_wk, L0_xattn_wv, L0_xattn_wo, L0_xattn_wk_ctx, L0_xattn_wv_ctx, L0_xattn_q_norm_w, L0_xattn_k_norm_w, L0_ffn_gate_w, L0_ffn_w_gate, L0_ffn_w_up, L0_ffn_w_down, L1_xattn_wq, L1_xattn_bq, L1_xattn_wkv, L1_xattn_bkv, L1_xattn_wp, L1_xattn_bp, L1_ffn_w_router, L1_ffn_w_gate, L1_ffn_w_up, L1_ffn_w_down, L1_ffn_amplitudes, L1_ffn_expert_scale, L1_ffn_shared_w_gate, L1_ffn_shared_w_up, L1_ffn_shared_w_down):
    import jax
    import jax.numpy as jnp

    def _L0_xattn_ref(x, h_ctx_kv, wq, wk, wv, wo, wk_ctx, wv_ctx, q_norm_w, k_norm_w):
        import jax, jax.numpy as jnp
        import numpy as np
        HIDDEN = 256
        NUM_HEADS = 16
        NUM_KV_HEADS = 4
        HEAD_DIM = 128
        ROPE_THETA = 10000.0
        EPS = 1e-06

        def rms_norm(x, w, eps=EPS):
            var = jnp.mean(jnp.square(x), axis=-1, keepdims=True)
            return x * jax.lax.rsqrt(var + eps) * w

        def rope_cache(L, head_dim, theta, dtype):
            inv_freq = 1.0 / theta ** (jnp.arange(0, head_dim, 2, dtype=jnp.float32) / head_dim)
            t = jnp.arange(L, dtype=jnp.float32)
            freqs = jnp.outer(t, inv_freq)
            emb = jnp.concatenate([freqs, freqs], -1)
            cos = jnp.cos(emb).astype(dtype)[None, :, None, :]
            sin = jnp.sin(emb).astype(dtype)[None, :, None, :]
            return (cos, sin)

        def rotate_half(x):
            x1, x2 = jnp.split(x, 2, axis=-1)
            return jnp.concatenate([-x2, x1], axis=-1)
        B, L, _ = x.shape
        T = h_ctx_kv.shape[1]
        rep = NUM_HEADS // NUM_KV_HEADS
        q = (x @ wq).reshape(B, L, NUM_HEADS, HEAD_DIM)
        k = (x @ wk).reshape(B, L, NUM_KV_HEADS, HEAD_DIM)
        v = (x @ wv).reshape(B, L, NUM_KV_HEADS, HEAD_DIM)
        q = rms_norm(q, q_norm_w)
        k = rms_norm(k, k_norm_w)
        k_ctx = (h_ctx_kv @ wk_ctx).reshape(B, T, NUM_KV_HEADS, HEAD_DIM)
        v_ctx = (h_ctx_kv @ wv_ctx).reshape(B, T, NUM_KV_HEADS, HEAD_DIM)
        k_ctx = rms_norm(k_ctx, k_norm_w)
        cos, sin = rope_cache(L, HEAD_DIM, ROPE_THETA, x.dtype)
        q = q * cos + rotate_half(q) * sin
        k = k * cos + rotate_half(k) * sin
        k_full = jnp.concatenate([k_ctx, k], axis=1)
        v_full = jnp.concatenate([v_ctx, v], axis=1)
        k_full = jnp.repeat(k_full, rep, axis=2)
        v_full = jnpp_repeat = jnp.repeat(v_full, rep, axis=2)
        i = jnp.arange(L)[:, None]
        j = jnp.arange(L)[None, :]
        causal = jnp.where(j > i, -jnp.inf, 0.0).astype(x.dtype)
        mask = jnp.concatenate([jnp.zeros((L, T), x.dtype), causal], axis=1)
        scale = 1.0 / np.sqrt(HEAD_DIM)
        scores = jnp.einsum('blhd,bmhd->bhlm', q, k_full) * scale + mask
        probs = jax.nn.softmax(scores, axis=-1)
        out = jnp.einsum('bhlm,bmhd->blhd', probs, v_full)
        out = out.reshape(B, L, NUM_HEADS * HEAD_DIM)
        return out @ wo

    def _L0_ffn_ref(hidden_states, gate_w, w_gate, w_up, w_down):
        import jax, jax.numpy as jnp
        import numpy as np
        B, S, D, FF, E = (4, 256, 256, 1024, 2)
        b, s, d = hidden_states.shape
        x = hidden_states.reshape(-1, d)
        logits = x @ gate_w.T
        probs = jax.nn.softmax(logits.astype(jnp.float32), axis=-1)
        sel = jnp.argmax(probs, axis=-1)
        top_w = jnp.take_along_axis(probs, sel[:, None], axis=-1)
        onehot = jax.nn.one_hot(sel, gate_w.shape[0], dtype=x.dtype)
        g = jnp.einsum('td,efd->etf', x, w_gate)
        u = jnp.einsum('td,efd->etf', x, w_up)
        h = jax.nn.silu(g) * u
        y = jnp.einsum('etf,edf->etd', h, w_down)
        out = jnp.einsum('etd,te->td', y, onehot * top_w)
        return out.reshape(b, s, d)

    def _L1_xattn_ref(x, cond, wq, bq, wkv, bkv, wp, bp):
        import jax, jax.numpy as jnp
        import numpy as np
        NUM_HEADS = 16

        def _qdq(x):
            s = jnp.maximum(jnp.max(jnp.abs(x), axis=-1, keepdims=True) / 127.0, 1e-08)
            return jnp.clip(jnp.round(x / s), -127.0, 127.0) * s
        B, N, C = x.shape
        M = cond.shape[1]
        H = NUM_HEADS
        Dh = C // H
        q = _qdq(x) @ _qdq(wq).T + bq
        kv = cond @ wkv.T + bkv
        k, v = jnp.split(kv, 2, axis=-1)
        q = q.reshape(B, N, H, Dh)
        k = k.reshape(B, M, H, Dh)
        v = v.reshape(B, M, H, Dh)
        scale = 1.0 / np.sqrt(Dh)
        attn = jax.nn.softmax(jnp.einsum('bnhd,bmhd->bhnm', q, k) * scale, axis=-1)
        o = jnp.einsum('bhnm,bmhd->bnhd', attn, v).reshape(B, N, C)
        out = _qdq(o) @ _qdq(wp).T + bp
        return out

    def _L1_ffn_ref(x, w_router, w_gate, w_up, w_down, amplitudes, expert_scale, shared_w_gate, shared_w_up, shared_w_down):
        import jax, jax.numpy as jnp
        import numpy as np
        H = 256
        I = 128
        K = 8
        E = 128
        TOPK = 4
        EPS = 1e-08
        B, S, _ = x.shape
        T = B * S
        xt = x.reshape(T, H)
        probs = jax.nn.softmax(xt @ w_router, axis=-1)
        topk_p, topk_idx = jax.lax.top_k(probs, TOPK)
        topk_w = topk_p / (jnp.sum(topk_p, axis=-1, keepdims=True) + EPS)
        gate = (xt @ w_gate).reshape(T, K, I)
        up = (xt @ w_up).reshape(T, K, I)
        basis = jax.nn.silu(gate) * up
        p = amplitudes[..., 0] ** 2 + amplitudes[..., 1] ** 2
        mix = p / (jnp.sum(p, axis=-1, keepdims=True) + EPS)
        mix_sel = mix[topk_idx]
        mixed = jnp.einsum('tek,tki->tei', mix_sel, basis)
        down = jnp.einsum('tei,ih->teh', mixed, w_down)
        coeff = topk_w * expert_scale[topk_idx]
        out = jnp.einsum('teh,te->th', down, coeff)
        shared = jax.nn.silu(xt @ shared_w_gate) * (xt @ shared_w_up) @ shared_w_down
        out = out + shared
        return out.reshape(B, S, H)
    x = x + jnp.tanh(g_xattn[0]) * _L0_xattn_ref(_layernorm(x, axis=-1), ctx_2048, L0_xattn_wq, L0_xattn_wk, L0_xattn_wv, L0_xattn_wo, L0_xattn_wk_ctx, L0_xattn_wv_ctx, L0_xattn_q_norm_w, L0_xattn_k_norm_w)
    x = x + jnp.tanh(g_ffn[0]) * _L0_ffn_ref(_layernorm(x, axis=-1), L0_ffn_gate_w, L0_ffn_w_gate, L0_ffn_w_up, L0_ffn_w_down)
    x = x + jnp.tanh(g_xattn[1]) * _L1_xattn_ref(_layernorm(x, axis=-1), ctx_2048, L1_xattn_wq, L1_xattn_bq, L1_xattn_wkv, L1_xattn_bkv, L1_xattn_wp, L1_xattn_bp)
    x = x + jnp.tanh(g_ffn[1]) * _L1_ffn_ref(_layernorm(x, axis=-1), L1_ffn_w_router, L1_ffn_w_gate, L1_ffn_w_up, L1_ffn_w_down, L1_ffn_amplitudes, L1_ffn_expert_scale, L1_ffn_shared_w_gate, L1_ffn_shared_w_up, L1_ffn_shared_w_down)
    return x

_drawn_inputs = setup_inputs


def setup_inputs(seed=0):
    import zlib

    import numpy as np

    out = dict(_drawn_inputs(seed))
    spreads = {'g_ffn': (-1.0, 0.6),
     'L0_xattn_q_norm_w': (1.0, 0.6),
     'L0_xattn_k_norm_w': (1.0, 0.6),
     'L1_ffn_expert_scale': (1.0, 0.6)}
    factors = {'L0_ffn_gate_w': 5.251,
     'L0_ffn_w_gate': 3.881,
     'L0_ffn_w_up': 3.842,
     'L0_ffn_w_down': 3.847,
     'L1_xattn_wq': 8.0,
     'L1_xattn_bq': 174.162,
     'L1_xattn_bkv': 8.0,
     'L1_xattn_bp': 3.022,
     'L1_ffn_w_router': 8.0,
     'L1_ffn_w_gate': 8.0,
     'L1_ffn_w_up': 8.0,
     'L1_ffn_w_down': 8.0,
     'L1_ffn_amplitudes': 8.0,
     'L1_ffn_shared_w_gate': 4.228,
     'L1_ffn_shared_w_up': 4.173,
     'L1_ffn_shared_w_down': 4.164}
    for name, (base, spread) in spreads.items():
        noise = np.random.default_rng([zlib.crc32(name.encode()), seed]).standard_normal(out[name].shape)
        drawn = base * np.exp(spread * noise) if base else spread * noise
        out[name] = jnp.asarray(drawn.astype(out[name].dtype))
    for name, factor in factors.items():
        out[name] = (out[name] * factor).astype(out[name].dtype)
    return out
```

```python
from contextlib import ExitStack

import numpy as np

import concourse.bass as bass
from concourse import mybir

F32 = mybir.dt.float32
F16 = mybir.dt.float16
BF16 = mybir.dt.bfloat16
I32 = mybir.dt.int32
U32 = mybir.dt.uint32
ALU = mybir.AluOpType
ACT = mybir.ActivationFunctionType
AX = mybir.AxisListType

B, L, T, DM = 8, 256, 64, 256
P = 128
KC = DM // P
NT = L // P
H, G, D = 16, 4, 128
HP = H // 2
KEYS = T + L
E0, FF = 2, 1024

WS = 64.0
PS = 1024.0
MASKED = -1e30
LN_EPS = 1e-5
RMS_EPS = 1e-6
RSQRT_MAGIC = float(0x5F3759DF)
LAST_PHASE = 4
HS = 4.0
ROUND = 1.5 * 2.0 ** 23
TG = 4
NG = B * NT // TG
FC = FF // P
E1, KB, I1 = 128, 8, 128
H1, D1 = 16, 16
HC = P // D1
EPS1 = 1e-8


def rep(ap2, n):
    p, m = ap2.shape
    return ap2.unsqueeze(1).broadcast_to([p, n, m])


def spread(ap2, m):
    p, n = ap2.shape
    return ap2.unsqueeze(2).broadcast_to([p, n, m])


def flamingo_layers(nc, x_in, ctxT_in, gates_in, consts, w0, out, last_phase=4):
    ctx = ExitStack()
    with ctx:
        def sb(name, shape, dt=F32):
            return ctx.enter_context(nc.sbuf_tensor(name, shape, dt))

        def sem(name):
            return ctx.enter_context(nc.semaphore(name))

        bQ, bS0, bS1, bR, bPa, bPb, bV, bM = (
            ctx.enter_context(nc.psum_tensor(n, [P, 512], F32))
            for n in ("bQ", "bS0", "bS1", "bR", "bPa", "bPb", "bV", "bM"))
        bS = [bS0, bS1]

        x = sb("x", [P, B * NT, DM])
        ctxT = sb("ctxT", [P, 2, KC, B * T], F16)
        ctxb = sb("ctxb", [P, 2, KC, 2, T], F16)
        ident = sb("ident", [P, P])
        identb = sb("identb", [P, P], BF16)
        maskb = sb("maskb", [P, P], BF16)
        ones = sb("ones", [P, 1])
        gates = sb("gates", [P, 4])
        tanhg = sb("tanhg", [P, 4])
        gscale = sb("gscale", [P, 4])
        cosT = sb("cosT", [P, L])
        sinT = sb("sinT", [P, L])
        cosR = sb("cosR", [P, NT, D])
        sinR = sb("sinR", [P, NT, D])
        qw = sb("qw", [P, 2])
        kw = sb("kw", [P, 2, D])
        gw0 = sb("gw0", [P, KC, E0])
        gw0p = sb("gw0p", [P, 2, KC, E0], F16)
        raw = sb("raw", [P, 3, 4096])
        parts = sb("parts", [P, 3, 2, 4096], F16)
        wkv = parts[:, 0].rearrange("p s (w k n) -> p s w k n", w=4, k=KC)
        wq = parts[:, 1].rearrange("p s (k n) -> p s k n", k=KC)
        wo = parts[:, 2].rearrange("p s (h n) -> p s h n", h=H)
        wg0 = parts[:, 0].rearrange("p s (e k n) -> p s e k n", e=E0, k=KC)
        wu0 = parts[:, 1].rearrange("p s (e k n) -> p s e k n", e=E0, k=KC)
        wd0 = parts[:, 2].rearrange("p s (e f n) -> p s e f n", e=E0, f=FC)
        flat = raw[:, :, :].rearrange("p a n -> p (a n)")
        flatp = parts[:, :, :, :].rearrange("p a s n -> p (a s n)")
        L1_COLS, n1 = {}, 0
        for name, width in (("kv", KC * 2 * DM), ("router", KC * E1), ("gate", KC * KB * I1), ("up", KC * KB * I1),
                            ("down", DM), ("sgate", KC * 2 * I1), ("sup", KC * 2 * I1), ("sdown", 2 * DM),
                            ("q", KC * DM), ("p", KC * DM)):
            L1_COLS[name] = (n1, width)
            n1 += width
        L1_ALL = n1
        L1_SPLIT = n1 - 2 * KC * DM

        def w1(name, k):
            at_, width = L1_COLS[name]
            return [flatp[:, j * L1_SPLIT + at_:j * L1_SPLIT + at_ + width].rearrange("p (k n) -> p k n", k=k)
                    for j in range(2)]

        outer = ctx
        ctx = ExitStack()
        stats = sb("stats", [P, NT, 6])
        mv = sb("mv", [P, NT, 2])
        nt0 = sb("nt0", [P, 16])
        nt1 = sb("nt1", [P, 16])
        rstd = sb("rstd", [P, NT])
        xn = sb("xn", [P, NT, DM])
        xT = sb("xT", [P, 2, KC, L], F16)
        sqk = sb("sqk", [P, 512])
        ssk = sb("ssk", [P, 3 * G])
        rk = sb("rk", [P, 3 * G])
        kr = sb("kr", [P, 3, G, D])
        ctx32 = kr[:, :, :, :].rearrange("p n g d -> p (n g d)")[:, 0:KC * B * T].rearrange("p (k n) -> p k n", k=KC)
        kT = sb("kT", [P, 2, G, KEYS], F16)
        v = sb("v", [P, 2, 3, G * D], F16)
        sq = sb("sq", [P, 512])
        qa = sb("qa", [P, 2, 2, L])
        qs = sb("qs", [P, 2, 2, L])
        ks = qs[:, :, :, :].rearrange("p a b n -> p a (b n)").rearrange("p a (g d) -> p a g d", g=G)
        qT = sb("qT", [P, 2, 2, 2, L], F16)
        rv = sb("rv", [P, 3, 4])
        ra = sb("ra", [P, 4])
        rq = sb("rq", [P, 3, 4])
        negmax = sb("negmax", [P, 2, 4])
        ebias = sb("ebias", [P, 2, 4])
        esum = sb("esum", [P, 2, 4])
        einv = sb("einv", [P, 2, 4])
        p = sb("p", [P, 2, 2, 512])
        kn = p[:, :, :, :].rearrange("p a b n -> p (a b n)")[:, 0:3 * G * D].rearrange("p (n g d) -> p n g d", n=3, g=G)
        pta = sb("pta", [P, 2, 2, 2, 4, P], F16)
        ptb = sb("ptb", [P, 2, 2, 2, 4, P], F16)
        oT = sb("oT", [P, 2, H, L], F16)
        ctx.close()
        ctx = outer

        gstats = sb("gstats", [P, TG, 6])
        gmv = sb("gmv", [P, TG, 2])
        gvar = sb("gvar", [P, TG])
        grstd = sb("grstd", [P, TG])
        gnt = sb("gnt", [P, 2, 8])
        gxn = sb("gxn", [P, TG, DM])
        gxT = sb("gxT", [P, 2, KC, TG * P], F16)
        lg = sb("lg", [P, TG, E0])
        ld = sb("ld", [P, TG])
        la = sb("la", [P, TG])
        lt = sb("lt", [P, TG])
        topw = sb("topw", [P, TG])
        cf = sb("cf", [P, E0, TG])
        cfg = sb("cfg", [P, E0, TG])
        sg = sb("sg", [P, 2, TG * P])
        hh32 = sb("hh32", [P, 2, TG * P])
        hT = sb("hT", [P, 4, 2, TG * P], F16)
        headmask = sb("headmask", [P, HC])
        keymask = sb("keymask", [P, 2])
        rows1 = sb("rows1", [P, 3, DM])
        bk = sb("bk", [P, KC])
        iota = sb("iota", [P, E1])
        onesM = sb("onesM", [P, P])
        wabs = sb("wabs", [P, 4])
        wsc = sb("wsc", [P, 4])
        winv = sb("winv", [P, 4])
        diag = sb("diag", [P, 4, P])
        srow = sb("srow", [P, 2, DM])
        wint = sb("wint", [P, 2, KC, DM], BF16)
        k1 = sb("k1", [P, KC, B * T])
        k1p = sb("k1p", [P, 2, KC, B * T], F16)
        kbd = sb("kbd", [P, 2, KC, HC, T], F16)
        ctxd = sb("ctxd", [P, 2, KC, 2, T], F16)
        v1 = sb("v1", [P, DM])
        vbd = sb("vbd", [P, 2, DM], F16)
        xabs = sb("xabs", [P, NT])
        xs = sb("xs", [P, NT])
        xsi = sb("xsi", [P, NT])
        xi = sb("xi", [P, NT, DM])
        xqT = sb("xqT", [P, KC, L], BF16)
        q1 = sb("q1", [P, NT, DM])
        q1T = sb("q1T", [P, 2, KC, L], F16)
        mx1 = sb("mx1", [P, 4, HC])
        e1 = sb("e1", [P, 4, HC, T])
        es1 = sb("es1", [P, 4, HC])
        ei1 = sb("ei1", [P, 4, HC])
        pt1 = sb("pt1", [P, 4, 2, 4, P], F16)
        oabs = sb("oabs", [P, NT])
        os1 = sb("os1", [P, NT])
        osi = sb("osi", [P, NT])
        y1 = q1
        amp = sb("amp", [P, KB, 2])
        mixp = sb("mixp", [P, KB])
        mixs = sb("mixs", [P, 2])
        escale = sb("escale", [P, 1])
        rmx = sb("rmx", [P, TG])
        rex = sb("rex", [P, TG, E1])
        rsum = sb("rsum", [P, TG])
        rinv = sb("rinv", [P, TG])
        top8 = sb("top8", [P, TG, 8])
        idx8 = sb("idx8", [P, TG, 8], U32)
        idxf = sb("idxf", [P, TG, 8])
        tw = sb("tw", [P, TG])
        chosen = sb("chosen", [P, TG, E1])
        WT = sb("WT", [P, TG * P])
        cc = sb("cc", [P, TG, KB])
        mixed = sb("mixed", [P, TG, I1])
        mT = sb("mT", [P, 2, TG * P], F16)

        names = """x_in x_rest_in ctx_in const_in w_in0 w_in1 w_in2 gw_hi gw_lo w_hi stage_free ctx_hi ctx_lo tables ones_ready
            gate_tanh gate_ready xn_ready xnT_mm xT_hi xT_lo kv_mm k_sq k_ssq kn_ready kr_ready kT_mm kT_hi kT_lo
            v_hi v_lo q_mm q_sq q_rope q_hi q_lo ssq_mm s_mm bias_ready ssq_read ctx_copy exp_done inv_ready p_norm pt_mm
            pt_hi pt_lo pv_mm o_hi o_lo wo_mm x_upd dve_step pool_step act_step stored pool_held l1_in c1_in lw_hi lw_lo
            a_wint a_wT a_wq a_diag a_srow a_srow_read a_k a_k1 a_khi a_klo
            a_x a_xT a_xq a_q a_q1 a_q1T a_qhi a_qlo a_kbd a_ctx a_v a_v1 a_vhi a_vlo a_s a_e a_exp a_inv a_p a_pt
            a_pthi a_ptlo a_o a_oi a_oT a_oq a_y a_upd
            r_mix r_logit r_e r_exp r_w r_wT r_wTc r_c r_cc m_g m_u m_silu m_h m_used m_hi m_lo m_mixed m_mT m_mhi m_mlo
            m_y m_upd 
            fw_hi fw_lo fx_ready fx_mm fx_hi fx_lo f_logit f_absd f_tanh f_coef fg_mm fu_mm f_silu f_h f_hhi f_hlo f_down  f_upd kc_mul ks_mul""".split()
        s = {n: sem(n) for n in names}

        block = ctx.enter_context(nc.Block())

        def product(pe, out_ap, lhsT, rhs, first, last):
            pe.matmul(out_ap, lhsT[0], rhs[0], start=first, stop=False, skip_group_check=True)
            pe.matmul(out_ap, lhsT[0], rhs[1], start=False, stop=False, skip_group_check=True)
            return pe.matmul(out_ap, lhsT[1], rhs[0], start=False, stop=last, skip_group_check=True)

        ROWS = [T, P, P]
        K_BANK = [bS0, bS1, bQ]
        V_BANK = [bR, bPa, bPb]
        V_ROWS = [2 * T, P, P]
        Q_BANK = [bQ, bR]
        COL = [0, T, T + P]
        KT_BANK = [bS0, bS1, bPa, bPb]
        SPAN = [T + P, T + L]
        AT = [0, T + P]


        @block.sync
        def _(sp):
            sp.dma_start(x[:, 0:NT, :], x_in[:, 0:NT, :]).then_inc(s["x_in"], 16)
            sp.dma_start(ctx32[:, :, :], ctxT_in).then_inc(s["ctx_in"], 16)
            sp.dma_start(raw[:, 0, :], w0["kv"]).then_inc(s["w_in0"], 16)
            for dst, name in ((ident, "ident"), (identb, "identb"), (maskb, "maskb"), (cosT, "cosT"), (sinT, "sinT"),
                              (cosR, "cosR"), (sinR, "sinR"), (qw, "qw"), (kw, "kw"), (gw0, "gw0")):
                sp.dma_start(dst[:], consts[name]).then_inc(s["const_in"], 16)
            sp.dma_start(gates[:, :], gates_in).then_inc(s["const_in"], 16)
            sp.dma_start(raw[:, 1, :], w0["q"]).then_inc(s["w_in1"], 16)
            sp.dma_start(raw[:, 2, :], w0["o"]).then_inc(s["w_in2"], 16)
            sp.dma_start(x[:, NT:B * NT, :], x_in[:, NT:B * NT, :]).then_inc(s["x_rest_in"], 16)
            for n, name in enumerate(("g", "u", "d")):
                sp.wait_ge(s["stage_free"], n + 1)
                sp.dma_start(raw[:, n, :], w0[name]).then_inc(s[f"w_in{n}"], 16)
            if last_phase == 1:
                sp.wait_ge(s["x_upd"], NT * B)
            if last_phase > 1:
                sp.wait_ge(s["x_upd"], NT * B)
                for dst, name in ((headmask, "headmask"), (keymask, "keymask"), (rows1, "rows1"), (bk, "bk"),
                                  (iota, "iota"), (amp, "amp"), (escale, "escale")):
                    sp.dma_start(dst[:], consts[name]).then_inc(s["c1_in"], 16)
                sp.wait_ge(s["fw_lo"], 3)
                sp.dma_start(flat[:, 0:L1_ALL], w0["l1"]).then_inc(s["l1_in"], 16)
            if last_phase == 2:
                sp.wait_ge(s["f_upd"], NG * TG * E0)
            if last_phase == 3:
                sp.wait_ge(s["a_upd"], B)
            if last_phase == 4:
                sp.wait_ge(s["m_upd"], NG * TG)
            sp.dma_start(out, x[:, :, :]).then_inc(s["stored"], 16)
            sp.wait_ge(s["stored"], 16)

        CONSTS = 11
        CONSTS1 = 7
        UNIT_S = [bS0, bS1, bPa, bPb]
        U1 = 10

        @block.scalar
        def _(act):
            def split_hi(n):
                act.wait_ge(s[f"w_in{n}"], 16)
                act.activation(parts[:, n, 0, :], raw[:, n, :], ACT.Copy, scale=WS).then_inc(s["w_hi"], 1)

            def tokens(b):
                act.wait_ge(s["xnT_mm"], b + 1)
                act.wait_ge(s["q_mm"], b * HP + 1)
                act.activation(xT[:, 0], bQ[:, :].rearrange("p (k n) -> p k n", k=KC), ACT.Copy)\
                   .then_inc(s["xT_hi"], 1)

            def key_squares(b):
                for n in range(3):
                    act.wait_ge(s["kv_mm"], b * 6 + n + 1)
                    if n:
                        act.wait_ge(s["k_ssq"], b * 3 + n)
                    act.activation(sqk[0:ROWS[n], :], K_BANK[n][0:ROWS[n], :], ACT.Square)\
                       .then_inc(s["k_sq"], 1)

            def values(b):
                for n in range(3):
                    act.wait_ge(s["kv_mm"], b * 6 + 3 + n + 1)
                    act.activation(v[0:V_ROWS[n], 0, n, :], V_BANK[n][0:V_ROWS[n], :], ACT.Copy)\
                       .then_inc(s["v_hi"], 1)

            def keys(b):
                for g in range(G):
                    act.wait_ge(s["kT_mm"], b * G + g + 1)
                    act.activation(kT[:, 0, g, :], KT_BANK[g][:, 0:KEYS], ACT.Copy).then_inc(s["kT_hi"], 1)

            def batch(b, following):
                def square(i):
                    act.wait_ge(s["q_rope"], b * HP + i + 1)
                    act.wait_ge(s["ssq_mm"], b * HP + i + 1)
                    act.activation(sq[:, :], Q_BANK[i % 2][:, :], ACT.Square).then_inc(s["q_sq"], 1)

                def exps(i):
                    act.wait_ge(s["pt_mm"], b * 2 * HP + 2 * i + 2)
                    for hh in range(2):
                        act.wait_ge(s["bias_ready"], b * H + 2 * i + hh + 1)
                        for t in range(NT):
                            j = 2 * hh + t
                            last = act.activation(
                                p[:, i % 2, hh, AT[t]:AT[t] + SPAN[t]], bS[hh][:, AT[t]:AT[t] + SPAN[t]], ACT.Exp,
                                bias=ebias[:, i % 2, j:j + 1], scale=rq[:, i % 3, j:j + 1],
                                accum_out=esum[:, i % 2, j:j + 1])
                        last.then_inc(s["exp_done"], 1)

                def probs_hi(i):
                    g, two = i // 2, slice(2 * (i % 2), 2 * (i % 2) + 2)
                    act.wait_ge(s["pv_mm"], b * 2 * G + 2 * g + 2)
                    for j, (dst, bank) in enumerate(((pta, bPa), (ptb, bPb))):
                        act.wait_ge(s["pt_mm"], b * 2 * HP + 2 * i + 4 + j + 1)
                        act.activation(dst[:, g % 2, 0, :, two, :],
                                       bank[:, :].rearrange("p (k h n) -> p k h n", k=2, h=2), ACT.Copy)\
                           .then_inc(s["pt_hi"], 1)

                def out_hi(g):
                    for t in range(NT):
                        act.wait_ge(s["pv_mm"], b * 2 * G + 2 * g + 4 + t + 1)
                        act.activation(oT[:, 0, 4 * g:4 * g + 4, t * P:(t + 1) * P],
                                       [bV, bM][t][:, :].rearrange("p (h n) -> p h n", h=4), ACT.Copy,
                                       scale=1.0 / PS).then_inc(s["o_hi"], 1)

                for i in range(HP + 4):
                    if 0 <= i - 2 < HP:
                        exps(i - 2)
                    if i < HP:
                        square(i)
                    if i == 0:
                        keys(b)
                    if 0 <= i - 3 < HP:
                        probs_hi(i - 3)
                    if i == HP and following:
                        tokens(b + 1)
                    if i == HP + 2 and following:
                        key_squares(b + 1)
                    if i >= 5 and i % 2 == 1:
                        out_hi((i - 5) // 2)
                if following:
                    values(b + 1)

            act.wait_ge(s["ctx_in"], 16)
            act.activation(ctxT[:, 0], ctx32[:, :, :], ACT.Copy).then_inc(s["ctx_hi"], 1)
            split_hi(0)
            tokens(0)
            key_squares(0)
            values(0)
            split_hi(1)
            split_hi(2)
            act.wait_ge(s["const_in"], 16 * CONSTS)
            act.activation(tanhg[:, :], gates[:, :], ACT.Tanh).then_inc(s["gate_tanh"], 1)
            act.activation(gw0p[:, 0], gw0[:, :, :], ACT.Copy, scale=WS).then_inc(s["gw_hi"], 1)
            with act.Fori(0, B - 1) as b:
                batch(b, True)
            batch(B - 1, False)
            if last_phase == 1:
                return

            act.wait_ge(s["x_upd"], B * NT)
            for n in range(3):
                act.wait_ge(s[f"w_in{n}"], 32)
                act.activation(parts[:, n, 0, :], raw[:, n, :], ACT.Copy, scale=WS).then_inc(s["fw_hi"], 1)

            def tokens_hi(c, first):
                for k in range(KC):
                    act.wait_ge(s["fx_mm"], first + c * KC + k + 1)
                    act.activation(gxT[:, 0, k], [bQ, bM][k][:, :], ACT.Copy).then_inc(s["fx_hi"], 1)

            def group0(c):
                tokens_hi(c, 0)
                act.wait_ge(s["f_absd"], c + 1)
                act.activation(lt[:, :], la[:, :], ACT.Tanh, scale=0.5).then_inc(s["f_tanh"], 1)
                U = E0 * FC
                for u in range(U + 1):
                    if u < U:
                        act.wait_ge(s["fg_mm"], c * U + u + 1)
                        act.wait_ge(s["f_h"], c * U + u + 1)
                        act.activation(sg[:, u % 2, :], bS[u % 2][:, :], ACT.Silu, scale=1.0 / WS)\
                           .then_inc(s["f_silu"], 1)
                    if u >= 1:
                        act.wait_ge(s["f_h"], c * U + u - 1 + 3)
                        act.wait_ge(s["f_down"], c * U + u - 1 + 1)
                        act.activation(hT[:, (u - 1) % 4, 0, :], hh32[:, (u - 1) % 2, :], ACT.Copy)\
                           .then_inc(s["f_hhi"], 1)

            with act.Fori(0, NG) as c:
                group0(c)
            if last_phase == 2:
                return

            act.wait_ge(s["f_upd"], NG * TG * E0)
            act.wait_ge(s["l1_in"], 16)
            act.activation(flatp[:, 0:L1_SPLIT], flat[:, 0:L1_SPLIT], ACT.Copy, scale=WS).then_inc(s["lw_hi"], 1)
            act.wait_ge(s["a_k1"], KC)
            act.activation(k1p[:, 0], k1[:, :, :], ACT.Copy).then_inc(s["a_khi"], 1)

            def batch1(b):
                act.wait_ge(s["a_v1"], b + 1)
                act.activation(vbd[:, 0, :], v1[:, :], ACT.Copy).then_inc(s["a_vhi"], 1)
                act.wait_ge(s["a_q1T"], b + 1)
                act.activation(q1T[:, 0], bM[:, :].rearrange("p (k n) -> p k n", k=KC), ACT.Copy)\
                   .then_inc(s["a_qhi"], 1)
                for u in range(4):
                    act.wait_ge(s["a_e"], 4 * b + u + 1)
                    act.activation(e1[:, u], e1[:, u], ACT.Exp, scale=float(D1) ** -0.5).then_inc(s["a_exp"], 1)
                for u in range(4):
                    act.wait_ge(s["a_pt"], 4 * b + u + 1)
                    act.activation(pt1[:, u, 0], [bR, bQ][u % 2][:, :].rearrange("p (m n) -> p m n", m=4), ACT.Copy)\
                       .then_inc(s["a_pthi"], 1)

            with act.Fori(0, B) as b:
                batch1(b)
            if last_phase == 3:
                return

            def group1(c):
                tokens_hi(c, NG * KC)
                act.wait_ge(s["r_e"], c + 1)
                act.activation(rex[:, :, :], rex[:, :, :], ACT.Exp, scale=1.0 / WS).then_inc(s["r_exp"], 1)
                for u in range(U1):
                    act.wait_ge(s["m_g"], c * U1 + u + 1)
                    act.wait_ge(s["m_h"], c * U1 + u + 1)
                    act.activation(sg[:, u % 2, :], bS[u % 2][:, :], ACT.Silu, scale=1.0 / WS).then_inc(s["m_silu"], 1)
                    if u < 2:
                        act.wait_ge(s["m_h"], c * U1 + u + 3)
                        act.activation(hT[:, u, 0, :], hh32[:, u % 2, :], ACT.Copy).then_inc(s["m_hi"], 1)
                act.wait_ge(s["m_mT"], c + 1)
                act.activation(mT[:, 0], bQ[:, :], ACT.Copy).then_inc(s["m_mhi"], 1)

            with act.Fori(0, NG) as c:
                group1(c)

        @block.vector
        def _(dve):
            count = [0]

            def mark(ins):
                count[0] += 1
                ins.then_inc(s["dve_step"], 1)
                return count[0]

            def step(ins):
                dve.wait_ge(s["dve_step"], mark(ins))

            def restart():
                dve.sem_clear(s["dve_step"])
                count[0] = 0

            def rsqrt(y, val, n, work=None):
                a = nt0[:, 0:n] if work is None else work
                step(dve.tensor_scalar(y.bitcast(I32), val.bitcast(I32), -0.5, RSQRT_MAGIC, ALU.mult, ALU.add))
                for _ in range(3):
                    step(dve.scalar_tensor_tensor(out=a, in0=y, scalar=-0.5, in1=val, op0=ALU.mult, op1=ALU.mult))
                    step(dve.tensor_tensor(a, a, y, ALU.mult))
                    step(dve.scalar_tensor_tensor(out=y, in0=a, scalar=1.5, in1=y, op0=ALU.add, op1=ALU.mult))

            def split_lo(n):
                dve.wait_ge(s["w_hi"], n + 1)
                dve.scalar_tensor_tensor(out=parts[:, n, 1, :], in0=raw[:, n, :], scalar=WS, in1=parts[:, n, 0, :],
                                         op0=ALU.mult, op1=ALU.subtract).then_inc(s["stage_free"], 1)

            def norm_tokens(b):
                for t in range(NT):
                    step(dve.bn_stats(stats[:, t, :], x[:, b * NT + t, :]))
                    step(dve.bn_aggr(mv[:, t, :], stats[:, t, :]))
                step(dve.tensor_scalar(nt1[:, 0:NT], mv[:, :, 1], LN_EPS, None, ALU.add))
                rsqrt(rstd[:, :], nt1[:, 0:NT], NT)
                for t in range(NT):
                    last = dve.tensor_scalar(xn[:, t, :], x[:, b * NT + t, :], mv[:, t, 0:1], rstd[:, t:t + 1],
                                             ALU.subtract, ALU.mult)
                last.then_inc(s["xn_ready"], 1)

            def tokens(b):
                dve.wait_ge(s["xT_hi"], b + 1)
                dve.tensor_tensor(xT[:, 1], bQ[:, :].rearrange("p (k n) -> p k n", k=KC), xT[:, 0], ALU.subtract)\
                   .then_inc(s["xT_lo"], 1)

            def key_norms(b):
                for n in range(3):
                    dve.wait_ge(s["k_sq"], b * 3 + n + 1)
                    dve.tensor_reduce(ssk[0:ROWS[n], n * G:(n + 1) * G],
                                      sqk[0:ROWS[n], :].rearrange("p (g d) -> p g d", g=G), AX.X, ALU.add)\
                       .then_inc(s["k_ssq"], 1)
                dve.wait_ge(s["k_ssq"], b * 3 + 3)
                step(dve.tensor_scalar(nt1[:, 0:3 * G], ssk[:, :], 1.0 / D, WS * WS * RMS_EPS, ALU.mult, ALU.add))
                rsqrt(rk[:, :], nt1[:, 0:3 * G], 3 * G)

            def scale_keys(b):
                for n in range(3):
                    r = ROWS[n]
                    dve.tensor_tensor(kn[0:r, n], K_BANK[n][0:r, :].rearrange("p (g d) -> p g d", g=G),
                                      spread(rk[0:r, n * G:(n + 1) * G], D), ALU.mult).then_inc(s["kn_ready"], 1)
                for n in range(1, 3):
                    dve.wait_ge(s["kn_ready"], b * 3 + n + 1)
                    for lo_, hi_ in ((0, D // 2), (D // 2, 0)):
                        last = dve.tensor_tensor(ks[:, n - 1, :, lo_:lo_ + D // 2], kn[:, n, :, hi_:hi_ + D // 2],
                                                 rep(sinR[:, n - 1, lo_:lo_ + D // 2], G), ALU.mult)
                    last.then_inc(s["ks_mul"], 1)

            def values(b):
                for n in range(3):
                    dve.wait_ge(s["v_hi"], b * 3 + n + 1)
                    dve.tensor_tensor(v[0:V_ROWS[n], 1, n, :], V_BANK[n][0:V_ROWS[n], :], v[0:V_ROWS[n], 0, n, :],
                                      ALU.subtract).then_inc(s["v_lo"], 1)

            def keys(b):
                for g in range(G):
                    dve.wait_ge(s["kT_hi"], b * G + g + 1)
                    dve.tensor_tensor(kT[:, 1, g, :], KT_BANK[g][:, 0:KEYS], kT[:, 0, g, :], ALU.subtract)\
                       .then_inc(s["kT_lo"], 1)

            def batch(b, following):
                done, stepped = {}, {}

                def newton(i, upto):
                    y, val = rq[:, i % 3, :], rv[:, i % 3, :]
                    for n in range(done[i], upto):
                        dve.wait_ge(s["dve_step"], stepped[i])
                        if n % 3 == 0:
                            ins = dve.scalar_tensor_tensor(out=ra[:, :], in0=y, scalar=-0.5, in1=val, op0=ALU.mult,
                                                           op1=ALU.mult)
                        elif n % 3 == 1:
                            ins = dve.tensor_tensor(ra[:, :], ra[:, :], y, ALU.mult)
                        else:
                            ins = dve.scalar_tensor_tensor(out=y, in0=ra[:, :], scalar=1.5, in1=y, op0=ALU.add,
                                                           op1=ALU.mult)
                        stepped[i] = mark(ins)
                    done[i] = max(done[i], upto)

                def rope(i):
                    q = Q_BANK[i % 2][:, :].rearrange("p (h n) -> p h n", h=2)
                    dve.wait_ge(s["q_mm"], b * HP + i + 2)
                    dve.wait_ge(s["q_lo"], b * HP + i + 1)
                    if i == 0:
                        dve.wait_ge(s["kr_ready"], b * 3 + 3)
                    half = D // 2
                    dve.tensor_tensor(qa[:, i % 2], q, rep(cosT[:, :], 2), ALU.mult)
                    if i:
                        newton(i - 1, 2)
                    dve.tensor_tensor(qs[0:half, i % 2], q[half:D], rep(sinT[0:half, :], 2), ALU.mult)
                    dve.tensor_tensor(qs[half:D, i % 2], q[0:half], rep(sinT[half:D, :], 2), ALU.mult)\
                       .then_inc(s["q_rope"], 1)

                def max_bias(i):
                    for hh in range(2):
                        dve.wait_ge(s["s_mm"], b * H + 2 * i + hh + 1)
                        for t in range(NT):
                            j = 2 * hh + t
                            newton(i, 6 + t)
                            last = dve.tensor_reduce(negmax[:, i % 2, j:j + 1],
                                                     bS[hh][:, AT[t]:AT[t] + SPAN[t]], AX.X, ALU.max, negate=True)
                        before = mark(last)
                        newton(i, 9)
                        dve.wait_ge(s["dve_step"], max(before, stepped[i]))
                        two = slice(2 * hh, 2 * hh + 2)
                        dve.tensor_tensor(ebias[:, i % 2, two], negmax[:, i % 2, two], rq[:, i % 3, two], ALU.mult)\
                           .then_inc(s["bias_ready"], 1)

                def norms(i):
                    dve.wait_ge(s["ssq_mm"], b * HP + i + 2)
                    dve.tensor_scalar(rv[:, i % 3, :], bM[:, 0:4], D * WS * WS * RMS_EPS, None, ALU.add)\
                       .then_inc(s["ssq_read"], 1)
                    dve.wait_ge(s["ssq_read"], b * HP + i + 1)
                    stepped[i] = mark(dve.tensor_scalar(rq[:, i % 3, :].bitcast(I32), rv[:, i % 3, :].bitcast(I32), -0.5,
                                                        RSQRT_MAGIC, ALU.mult, ALU.add))
                    done[i] = 0

                def inverse(i):
                    dve.wait_ge(s["exp_done"], b * H + 2 * i + 2)
                    dve.reciprocal(einv[:, i % 2, :], esum[:, i % 2, :]).then_inc(s["inv_ready"], 1)

                def probs_lo(i):
                    g, two = i // 2, slice(2 * (i % 2), 2 * (i % 2) + 2)
                    for j, (dst, bank) in enumerate(((pta, bPa), (ptb, bPb))):
                        dve.wait_ge(s["pt_hi"], b * 2 * HP + 2 * i + j + 1)
                        dve.tensor_tensor(dst[:, g % 2, 1, :, two, :],
                                          bank[:, :].rearrange("p (k h n) -> p k h n", k=2, h=2),
                                          dst[:, g % 2, 0, :, two, :], ALU.subtract).then_inc(s["pt_lo"], 1)

                def out_lo(g):
                    for t in range(NT):
                        dve.wait_ge(s["o_hi"], b * 2 * G + 2 * g + t + 1)
                        heads, cols = slice(4 * g, 4 * g + 4), slice(t * P, (t + 1) * P)
                        dve.scalar_tensor_tensor(out=oT[:, 1, heads, cols],
                                                 in0=[bV, bM][t][:, :].rearrange("p (h n) -> p h n", h=4),
                                                 scalar=1.0 / PS, in1=oT[:, 0, heads, cols],
                                                 op0=ALU.mult, op1=ALU.subtract).then_inc(s["o_lo"], 1)

                for i in range(HP + 4):
                    if 0 <= i - 2 < HP:
                        max_bias(i - 2)
                    if 1 <= i <= HP:
                        norms(i - 1)
                        newton(i - 1, 1)
                    if i < HP:
                        rope(i)
                    if i == 0:
                        keys(b)
                    if 1 <= i <= HP:
                        newton(i - 1, 3)
                    if 0 <= i - 2 < HP:
                        inverse(i - 2)
                    if 1 <= i <= HP:
                        newton(i - 1, 4)
                    if 0 <= i - 3 < HP:
                        probs_lo(i - 3)
                    if i == HP - 2 and following:
                        norm_tokens(b + 1)
                    if i == HP and following:
                        tokens(b + 1)
                    if i == HP + 2 and following:
                        key_norms(b + 1)
                    if i >= 5 and i % 2 == 1:
                        out_lo((i - 5) // 2)
                if following:
                    scale_keys(b + 1)
                    values(b + 1)
                for t in range(NT):
                    dve.wait_ge(s["wo_mm"], b * NT + t + 1)
                    dve.scalar_tensor_tensor(out=x[:, b * NT + t, :], in0=[bV, bM][t][:, 0:DM],
                                             scalar=gscale[:, 0:1], in1=x[:, b * NT + t, :],
                                             op0=ALU.mult, op1=ALU.add).then_inc(s["x_upd"], 1)
                restart()

            dve.memset(ones[:, :], 1.0).then_inc(s["ones_ready"], 1)
            step(dve.memset(ssk[:, :], 1.0))
            dve.wait_ge(s["x_in"], 16)
            norm_tokens(0)
            dve.wait_ge(s["ctx_hi"], 1)
            dve.tensor_tensor(ctxT[:, 1], ctx32[:, :, :], ctxT[:, 0], ALU.subtract).then_inc(s["ctx_lo"], 1)
            split_lo(0)
            dve.wait_ge(s["const_in"], 16 * CONSTS)
            step(dve.tensor_scalar(cosT[:, :], cosT[:, :], qw[:, 0:1], None, ALU.mult))
            step(dve.tensor_scalar(sinT[:, :], sinT[:, :], qw[:, 1:2], None, ALU.mult))
            step(dve.tensor_tensor(cosR[:, :, :], cosR[:, :, :], rep(kw[:, 0, :], NT), ALU.mult))
            step(dve.tensor_tensor(sinR[:, :, :], sinR[:, :, :], rep(kw[:, 1, :], NT), ALU.mult))
            tokens(0)
            key_norms(0)
            scale_keys(0)
            values(0)
            split_lo(1)
            split_lo(2)
            dve.wait_ge(s["gate_tanh"], 1)
            step(dve.tensor_scalar(gscale[:, 0:1], tanhg[:, 0:1], 1.0 / (WS * WS), None, ALU.mult))
            step(dve.tensor_scalar(gscale[:, 2:4], tanhg[:, 2:4], 1.0 / (WS * HS), None, ALU.mult))
            dve.wait_ge(s["gw_hi"], 1)
            dve.scalar_tensor_tensor(out=gw0p[:, 1], in0=gw0[:, :, :], scalar=WS, in1=gw0p[:, 0],
                                     op0=ALU.mult, op1=ALU.subtract).then_inc(s["gw_lo"], 1)
            dve.wait_ge(s["x_rest_in"], 16)
            restart()
            with dve.Fori(0, B - 1) as b:
                batch(b, True)
            batch(B - 1, False)
            if last_phase == 1:
                return

            dve.wait_ge(s["x_upd"], B * NT)
            dve.sem_inc(s["f_h"], 2)
            for n in range(3):
                dve.wait_ge(s["fw_hi"], n + 1)
                dve.scalar_tensor_tensor(out=parts[:, n, 1, :], in0=raw[:, n, :], scalar=WS, in1=parts[:, n, 0, :],
                                         op0=ALU.mult, op1=ALU.subtract).then_inc(s["fw_lo"], 1)

            def layer_norm(c):
                for t in range(TG):
                    step(dve.bn_stats(gstats[:, t, :], x[:, c * TG + t, :]))
                    step(dve.bn_aggr(gmv[:, t, :], gstats[:, t, :]))
                step(dve.tensor_scalar(gvar[:, :], gmv[:, :, 1], LN_EPS, None, ALU.add))
                rsqrt(grstd[:, :], gvar[:, :], TG, work=gnt[:, 0, 0:TG])
                for t in range(TG):
                    last = dve.tensor_scalar(gxn[:, t, :], x[:, c * TG + t, :], gmv[:, t, 0:1], grstd[:, t:t + 1],
                                             ALU.subtract, ALU.mult)
                last.then_inc(s["fx_ready"], 1)

            def tokens_lo(c, first):
                for k in range(KC):
                    dve.wait_ge(s["fx_hi"], first + c * KC + k + 1)
                    dve.tensor_tensor(gxT[:, 1, k], [bQ, bM][k][:, :], gxT[:, 0, k], ALU.subtract)\
                       .then_inc(s["fx_lo"], 1)

            def group0(c):
                layer_norm(c)
                tokens_lo(c, 0)
                dve.wait_ge(s["f_logit"], c + 1)
                step(dve.tensor_scalar(lg[:, :, :], bM[:, 0:TG * E0].rearrange("p (t e) -> p t e", t=TG), 1.0 / WS, None,
                                       ALU.mult))
                step(dve.tensor_tensor(ld[:, :], lg[:, :, 0], lg[:, :, 1], ALU.subtract))
                step(dve.tensor_scalar(lt[:, :], ld[:, :], -1.0, None, ALU.mult))
                dve.tensor_tensor(la[:, :], ld[:, :], lt[:, :], ALU.max).then_inc(s["f_absd"], 1)
                dve.wait_ge(s["f_tanh"], c + 1)
                step(dve.tensor_scalar(topw[:, :], lt[:, :], 0.5, 0.5, ALU.mult, ALU.add))
                step(dve.scalar_tensor_tensor(out=cf[:, 0, :], in0=ld[:, :], scalar=0.0, in1=topw[:, :],
                                              op0=ALU.is_ge, op1=ALU.mult))
                step(dve.tensor_tensor(cf[:, 1, :], topw[:, :], cf[:, 0, :], ALU.subtract))
                step(dve.tensor_scalar(cfg[:, :, :], cf[:, :, :], gscale[:, 2:3], None, ALU.mult))
                U = E0 * FC
                for u in range(U + 3):
                    if u < U:
                        dve.wait_ge(s["f_silu"], c * U + u + 1)
                        dve.wait_ge(s["fu_mm"], c * U + u + 1)
                        if u >= 2:
                            dve.wait_ge(s["f_hlo"], c * U + u - 1)
                        dve.scalar_tensor_tensor(out=hh32[:, u % 2, :], in0=[bPa, bPb][u % 2][:, :], scalar=HS / WS,
                                                 in1=sg[:, u % 2, :], op0=ALU.mult, op1=ALU.mult).then_inc(s["f_h"], 1)
                    if 1 <= u <= U:
                        dve.wait_ge(s["f_hhi"], c * U + u)
                        dve.tensor_tensor(hT[:, (u - 1) % 4, 1, :], hh32[:, (u - 1) % 2, :], hT[:, (u - 1) % 4, 0, :],
                                          ALU.subtract).then_inc(s["f_hlo"], 1)
                    if u - 2 in (FC - 1, U - 1):
                        e = (u - 2) // FC
                        dve.wait_ge(s["f_down"], c * U + e * FC + FC + 4)
                        for t in range(TG):
                            if e:
                                dve.wait_ge(s["f_upd"], c * TG * E0 + t + 1)
                            y = [bV, bR][t // 2][:, (t % 2) * DM:(t % 2 + 1) * DM]
                            dve.scalar_tensor_tensor(out=x[:, c * TG + t, :], in0=y, scalar=cfg[:, e, t:t + 1],
                                                     in1=x[:, c * TG + t, :], op0=ALU.mult, op1=ALU.add)\
                               .then_inc(s["f_upd"], 1)
                restart()

            with dve.Fori(0, NG) as c:
                group0(c)
            if last_phase == 2:
                return

            def whole(out_ap, in_ap, inverse_scale):
                step(dve.tensor_scalar(out_ap, in_ap, inverse_scale, ROUND, ALU.mult, ALU.add))
                step(dve.tensor_scalar(out_ap, out_ap, ROUND, 127.0, ALU.subtract, ALU.min))

            dve.wait_ge(s["f_upd"], NG * TG * E0)
            dve.wait_ge(s["c1_in"], 16 * CONSTS1)
            dve.wait_ge(s["l1_in"], 16)
            step(dve.tensor_copy(gscale[:, 1:2], tanhg[:, 1:2]))
            step(dve.memset(onesM[:, :], 1.0))
            wqp = flat[:, L1_SPLIT:L1_ALL].rearrange("p (j n) -> p j n", j=4)
            step(dve.tensor_reduce(wabs[:, :], wqp, AX.X, ALU.max, apply_absolute_value=True))
            step(dve.tensor_scalar(wsc[:, :], wabs[:, :], 1.0 / 127.0, 1e-8, ALU.mult, ALU.max))
            step(dve.reciprocal(winv[:, :], wsc[:, :]))
            for j in range(4):
                whole(wqp[:, j], wqp[:, j], winv[:, j:j + 1])
                last = dve.tensor_scalar(diag[:, j], ident[:, :], wsc[:, j:j + 1], None, ALU.mult)
            last.then_inc(s["a_wint"], 1)
            for j in range(2):
                dve.wait_ge(s["a_wT"], j + 1)
                dve.tensor_scalar(wint[:, j], [bS0, bS1][j][:, :].rearrange("p (k n) -> p k n", k=KC), -127.0, None,
                                  ALU.max).then_inc(s["a_wq"], 1)
            dve.wait_ge(s["a_srow"], 1)
            dve.tensor_copy(srow[:, :, :], bPa[:, :].rearrange("p (j n) -> p j n", j=2)).then_inc(s["a_srow_read"], 1)
            dve.wait_ge(s["lw_hi"], 1)
            dve.scalar_tensor_tensor(out=flatp[:, L1_SPLIT:2 * L1_SPLIT], in0=flat[:, 0:L1_SPLIT], scalar=WS,
                                     in1=flatp[:, 0:L1_SPLIT], op0=ALU.mult, op1=ALU.subtract).then_inc(s["lw_lo"], 1)
            for k in range(KC):
                dve.wait_ge(s["a_k"], k + 1)
                dve.tensor_scalar(k1[:, k], [bPb, bR][k][:, :], 1.0 / WS, bk[:, k:k + 1], ALU.mult, ALU.add)\
                   .then_inc(s["a_k1"], 1)
            dve.wait_ge(s["a_khi"], 1)
            dve.tensor_tensor(k1p[:, 1], k1[:, :, :], k1p[:, 0], ALU.subtract).then_inc(s["a_klo"], 1)
            step(dve.tensor_tensor(amp[:, :, :], amp[:, :, :], amp[:, :, :], ALU.mult))
            step(dve.tensor_reduce(mixp[:, :], amp[:, :, :], AX.X, ALU.add))
            step(dve.tensor_reduce(mixs[:, 0:1], mixp[:, :], AX.X, ALU.add))
            step(dve.tensor_scalar(mixs[:, 0:1], mixs[:, 0:1], EPS1, None, ALU.add))
            step(dve.reciprocal(mixs[:, 1:2], mixs[:, 0:1]))
            dve.tensor_scalar(mixp[:, :], mixp[:, :], mixs[:, 1:2], escale[:, 0:1], ALU.mult, ALU.mult)\
               .then_inc(s["r_mix"], 1)
            dve.wait_ge(s["r_mix"], 1)
            dve.wait_ge(s["a_srow_read"], 1)
            restart()

            def batch1(b):
                for t in range(NT):
                    step(dve.bn_stats(gstats[:, t, :], x[:, b * NT + t, :]))
                    step(dve.bn_aggr(gmv[:, t, :], gstats[:, t, :]))
                step(dve.tensor_scalar(gvar[:, 0:NT], gmv[:, 0:NT, 1], LN_EPS, None, ALU.add))
                rsqrt(grstd[:, 0:NT], gvar[:, 0:NT], NT, work=gnt[:, 0, 0:NT])
                for t in range(NT):
                    step(dve.tensor_scalar(gxn[:, t, :], x[:, b * NT + t, :], gmv[:, t, 0:1], grstd[:, t:t + 1],
                                           ALU.subtract, ALU.mult))
                step(dve.tensor_reduce(xabs[:, :], gxn[:, 0:NT, :], AX.X, ALU.max, apply_absolute_value=True))
                step(dve.tensor_scalar(xs[:, :], xabs[:, :], 1.0 / 127.0, 1e-8, ALU.mult, ALU.max))
                step(dve.reciprocal(xsi[:, :], xs[:, :]))
                for t in range(NT):
                    step(dve.tensor_scalar(xi[:, t], gxn[:, t, :], xsi[:, t:t + 1], ROUND, ALU.mult, ALU.add))
                dve.tensor_scalar(xi[:, :, :], xi[:, :, :], ROUND, 127.0, ALU.subtract, ALU.min).then_inc(s["a_x"], 1)
                dve.wait_ge(s["a_xT"], b + 1)
                dve.tensor_scalar(xqT[:, :, :], bM[:, :].rearrange("p (k n) -> p k n", k=KC), -127.0, None, ALU.max)\
                   .then_inc(s["a_xq"], 1)
                dve.wait_ge(s["a_v"], b + 1)
                step(dve.scalar_tensor_tensor(out=v1[:, :], in0=bV[:, 0:DM], scalar=1.0 / WS, in1=rows1[:, 2, :],
                                              op0=ALU.mult, op1=ALU.add))
                vv = v1[:, :].rearrange("p (m s d) -> p m s d", m=H1 // 2, s=2)
                for half in range(2):
                    last = dve.tensor_scalar(vv[:, :, half], vv[:, :, half], keymask[:, half:half + 1], None, ALU.mult)
                last.then_inc(s["a_v1"], 1)
                dve.wait_ge(s["a_q"], b + 1)
                for t in range(NT):
                    step(dve.scalar_tensor_tensor(out=q1[:, t], in0=bQ[:, t * DM:(t + 1) * DM], scalar=xs[:, t:t + 1],
                                                  in1=srow[:, 0, :], op0=ALU.mult, op1=ALU.mult))
                dve.tensor_tensor(q1[:, :, :], q1[:, :, :], rep(rows1[:, 0, :], NT), ALU.add).then_inc(s["a_q1"], 1)
                dve.wait_ge(s["a_vhi"], b + 1)
                dve.tensor_tensor(vbd[:, 1, :], v1[:, :], vbd[:, 0, :], ALU.subtract).then_inc(s["a_vlo"], 1)
                dve.wait_ge(s["a_qhi"], b + 1)
                dve.tensor_tensor(q1T[:, 1], bM[:, :].rearrange("p (k n) -> p k n", k=KC), q1T[:, 0], ALU.subtract)\
                   .then_inc(s["a_qlo"], 1)
                for u in range(4):
                    sc = UNIT_S[u][:, :].rearrange("p (h n) -> p h n", h=HC)
                    dve.wait_ge(s["a_s"], 4 * b + u + 1)
                    step(dve.tensor_reduce(mx1[:, u, :], sc, AX.X, ALU.max))
                    dve.tensor_tensor(e1[:, u], sc, spread(mx1[:, u, :], T), ALU.subtract).then_inc(s["a_e"], 1)
                for u in range(4):
                    dve.wait_ge(s["a_exp"], 4 * b + u + 1)
                    step(dve.tensor_reduce(es1[:, u, :], e1[:, u], AX.X, ALU.add))
                    step(dve.reciprocal(ei1[:, u, :], es1[:, u, :]))
                    dve.tensor_scalar(ei1[:, u, :], ei1[:, u, :], PS, None, ALU.mult).then_inc(s["a_inv"], 1)
                for u in range(4):
                    dve.wait_ge(s["a_pthi"], 4 * b + u + 1)
                    dve.tensor_tensor(pt1[:, u, 1], [bR, bQ][u % 2][:, :].rearrange("p (m n) -> p m n", m=4),
                                      pt1[:, u, 0], ALU.subtract).then_inc(s["a_ptlo"], 1)
                for t in range(NT):
                    dve.wait_ge(s["a_o"], NT * b + t + 1)
                    step(dve.tensor_reduce(oabs[:, t:t + 1], [bV, bM][t][:, 0:DM], AX.X, ALU.max,
                                           apply_absolute_value=True))
                step(dve.tensor_scalar(os1[:, :], oabs[:, :], 1.0 / 127.0, PS * 1e-8, ALU.mult, ALU.max))
                step(dve.reciprocal(osi[:, :], os1[:, :]))
                for t in range(NT):
                    step(dve.tensor_scalar(xi[:, t], [bV, bM][t][:, 0:DM], osi[:, t:t + 1], ROUND, ALU.mult, ALU.add))
                dve.tensor_scalar(xi[:, :, :], xi[:, :, :], ROUND, 127.0, ALU.subtract, ALU.min).then_inc(s["a_oi"], 1)
                step(dve.tensor_scalar(os1[:, :], os1[:, :], 1.0 / PS, None, ALU.mult))
                dve.wait_ge(s["a_oT"], b + 1)
                dve.tensor_scalar(xqT[:, :, :], bR[:, :].rearrange("p (k n) -> p k n", k=KC), -127.0, None, ALU.max)\
                   .then_inc(s["a_oq"], 1)
                dve.wait_ge(s["a_y"], b + 1)
                for t in range(NT):
                    step(dve.scalar_tensor_tensor(out=y1[:, t], in0=bQ[:, t * DM:(t + 1) * DM], scalar=os1[:, t:t + 1],
                                                  in1=srow[:, 1, :], op0=ALU.mult, op1=ALU.mult))
                step(dve.tensor_tensor(y1[:, :, :], y1[:, :, :], rep(rows1[:, 1, :], NT), ALU.add))
                xb = x[:, bass.ds(b * NT, NT), :].rearrange("p t n -> p (t n)")
                dve.scalar_tensor_tensor(out=xb, in0=y1[:, :, :].rearrange("p t n -> p (t n)"), scalar=gscale[:, 1:2],
                                         in1=xb, op0=ALU.mult, op1=ALU.add).then_inc(s["a_upd"], 1)
                restart()

            with dve.Fori(0, B) as b:
                batch1(b)
            if last_phase == 3:
                return

            dve.wait_ge(s["a_upd"], B)
            dve.sem_inc(s["m_h"], 2)

            def group1(c):
                layer_norm(c)
                tokens_lo(c, NG * KC)
                lgt = bR[:, :].rearrange("p (t e) -> p t e", t=TG)
                dve.wait_ge(s["r_logit"], c + 1)
                step(dve.tensor_reduce(rmx[:, :], lgt, AX.X, ALU.max))
                dve.tensor_tensor(rex[:, :, :], lgt, spread(rmx[:, :], E1), ALU.subtract).then_inc(s["r_e"], 1)
                dve.wait_ge(s["r_exp"], c + 1)
                step(dve.tensor_reduce(rsum[:, :], rex[:, :, :], AX.X, ALU.add))
                step(dve.reciprocal(rinv[:, :], rsum[:, :]))
                step(dve.tensor_tensor(rex[:, :, :], rex[:, :, :], spread(rinv[:, :], E1), ALU.mult))
                for t in range(TG):
                    last = dve.max(top8[:, t, :], rex[:, t, :])
                step(last)
                for t in range(TG):
                    last = dve.max_index(idx8[:, t, :], top8[:, t, :], rex[:, t, :])
                step(last)
                step(dve.tensor_copy(idxf[:, :, :], idx8[:, :, :]))
                step(dve.tensor_reduce(tw[:, :], top8[:, :, 0:4], AX.X, ALU.add))
                step(dve.tensor_scalar(tw[:, :], tw[:, :], EPS1, None, ALU.add))
                step(dve.reciprocal(tw[:, :], tw[:, :]))
                for k in range(4):
                    for t in range(TG):
                        if k == 0:
                            last = dve.tensor_scalar(chosen[:, t, :], iota[:, :], idxf[:, t, 0:1], None, ALU.is_equal)
                        else:
                            last = dve.scalar_tensor_tensor(out=chosen[:, t, :], in0=iota[:, :],
                                                            scalar=idxf[:, t, k:k + 1], in1=chosen[:, t, :],
                                                            op0=ALU.is_equal, op1=ALU.add)
                    step(last)
                for t in range(TG):
                    last = dve.scalar_tensor_tensor(out=chosen[:, t, :], in0=chosen[:, t, :], scalar=tw[:, t:t + 1],
                                                    in1=rex[:, t, :], op0=ALU.mult, op1=ALU.mult)
                last.then_inc(s["r_w"], 1)
                dve.wait_ge(s["r_wT"], c + 1)
                dve.tensor_copy(WT[:, :], bR[:, :]).then_inc(s["r_wTc"], 1)
                dve.wait_ge(s["r_c"], c + 1)
                dve.tensor_copy(cc[:, :, :], bM[:, 0:TG * KB].rearrange("p (t k) -> p t k", t=TG)).then_inc(s["r_cc"], 1)
                dve.wait_ge(s["r_cc"], c + 1)
                for u in range(U1):
                    dve.wait_ge(s["m_silu"], c * U1 + u + 1)
                    dve.wait_ge(s["m_u"], c * U1 + u + 1)
                    dve.scalar_tensor_tensor(out=hh32[:, u % 2, :], in0=[bPa, bPb][u % 2][:, :], scalar=HS / WS,
                                             in1=sg[:, u % 2, :], op0=ALU.mult, op1=ALU.mult).then_inc(s["m_h"], 1)
                    if u < 2:
                        dve.wait_ge(s["m_hi"], c * 2 + u + 1)
                        step(dve.tensor_tensor(hT[:, u, 1, :], hh32[:, u % 2, :], hT[:, u, 0, :], ALU.subtract))
                        continue
                    dve.wait_ge(s["m_h"], c * U1 + u + 3)
                    t, half = (u - 2) // 2, (u - 2) % 2
                    for k in range(4):
                        base = hh32[:, u % 2, k * I1:(k + 1) * I1]
                        w = cc[:, t, half * 4 + k:half * 4 + k + 1]
                        if half == 0 and k == 0:
                            step(dve.tensor_scalar(mixed[:, t, :], base, w, None, ALU.mult))
                        else:
                            last = dve.scalar_tensor_tensor(out=mixed[:, t, :], in0=base, scalar=w, in1=mixed[:, t, :],
                                                            op0=ALU.mult, op1=ALU.add)
                            if u == U1 - 1 and k == 3:
                                last.then_inc(s["m_mixed"], 1)
                            else:
                                step(last)
                dve.wait_ge(s["m_mhi"], c + 1)
                dve.tensor_tensor(mT[:, 1], bQ[:, :], mT[:, 0], ALU.subtract).then_inc(s["m_mlo"], 1)
                for t in range(TG):
                    dve.wait_ge(s["m_y"], c * 2 + t // 2 + 1)
                    dve.scalar_tensor_tensor(out=x[:, c * TG + t, :],
                                             in0=[bV, bM][t // 2][:, (t % 2) * DM:(t % 2 + 1) * DM],
                                             scalar=gscale[:, 3:4], in1=x[:, c * TG + t, :],
                                             op0=ALU.mult, op1=ALU.add).then_inc(s["m_upd"], 1)
                restart()

            with dve.Fori(0, NG) as c:
                group1(c)

        @block.gpsimd
        def _(pool):
            pool.sem_inc(s["q_lo"], 2)

            pool.wait_ge(s["ctx_lo"], 1)

            def hold():
                pool.sem_inc(s["pool_held"], 1)

            def context(b):
                for half in range(2):
                    last = pool.tensor_copy(ctxb[:, :, :, half, :], ctxT[:, :, :, bass.ds(b * T, T)])
                last.then_inc(s["ctx_copy"], 1)

            def keys(b):
                for n in range(3):
                    r = ROWS[n]
                    pool.wait_ge(s["kn_ready"], b * 3 + n + 1)
                    if n == 0:
                        pool.tensor_tensor(kr[0:r, n], kn[0:r, n], rep(kw[0:r, 0, :], G), ALU.mult)\
                            .then_inc(s["kr_ready"], 1)
                    else:
                        pool.tensor_tensor(kr[:, n], kn[:, n], rep(cosR[:, n - 1, :], G), ALU.mult)\
                            .then_inc(s["kc_mul"], 1)
                        pool.wait_ge(s["ks_mul"], b * 2 + n)
                        pool.wait_ge(s["kc_mul"], b * 2 + n)
                        pool.tensor_tensor(kr[:, n], kr[:, n], ks[:, n - 1], ALU.add).then_inc(s["kr_ready"], 1)

            def batch(b, following):
                def rope(i):
                    j = i % 2
                    pool.wait_ge(s["q_rope"], b * HP + i + 1)
                    pool.tensor_tensor(qa[:, j], qa[:, j], qs[:, j], ALU.add).then_inc(s["pool_step"], 1)
                    pool.wait_ge(s["pool_step"], b * HP + i + 1)
                    if i >= 2:
                        pool.wait_ge(s["s_mm"], b * H + 2 * (i - 2) + 2)
                    hold()
                    pool.tensor_scalar(qT[:, j, 0], qa[:, j], 1.0, 1.0, ALU.mult, ALU.mult).then_inc(s["q_hi"], 1)
                    pool.wait_ge(s["q_hi"], b * HP + i + 1)
                    pool.tensor_tensor(qT[:, j, 1], qa[:, j], qT[:, j, 0], ALU.subtract).then_inc(s["q_lo"], 1)

                def normalise(i):
                    pool.wait_ge(s["inv_ready"], b * HP + i + 1)
                    hold()
                    for hh in range(2):
                        for t in range(NT):
                            a = p[:, i % 2, hh, AT[t]:AT[t] + SPAN[t]]
                            last = pool.tensor_scalar(a, a, einv[:, i % 2, 2 * hh + t:2 * hh + t + 1], PS,
                                                      ALU.mult, ALU.mult)
                    last.then_inc(s["p_norm"], 1)

                for i in range(HP + 2):
                    if i >= 2:
                        normalise(i - 2)
                    if i < HP:
                        rope(i)
                    if i == HP and following:
                        context(b + 1)
                if following:
                    keys(b + 1)

            context(0)
            keys(0)
            with pool.Fori(0, B - 1) as b:
                batch(b, True)
            batch(B - 1, False)
            if last_phase < 3:
                return

            pool.wait_ge(s["a_klo"], 1)

            def batch1(b):
                for j in range(2):
                    for rpt in range(2):
                        last = pool.tensor_copy(ctxd[:, j, :, rpt, :], ctxT[:, j, :, bass.ds(b * T, T)])
                last.then_inc(s["a_ctx"], 1)
                for j in range(2):
                    for k in range(KC):
                        last = pool.tensor_tensor(kbd[:, j, k], rep(k1p[:, j, k, bass.ds(b * T, T)], HC),
                                                  spread(headmask[:, :], T), ALU.mult)
                last.then_inc(s["a_kbd"], 1)
                for u in range(4):
                    pool.wait_ge(s["a_inv"], 4 * b + u + 1)
                    pool.tensor_tensor(e1[:, u], e1[:, u], spread(ei1[:, u, :], T), ALU.mult).then_inc(s["a_p"], 1)

            with pool.Fori(0, B) as b:
                batch1(b)

        @block.tensor
        def _(pe):
            pe.sem_inc(s["q_mm"], 1)
            pe.sem_inc(s["ssq_mm"], 1)
            pe.sem_inc(s["pt_mm"], 4)
            pe.sem_inc(s["pv_mm"], 4)
            pe.wait_ge(s["const_in"], 16 * CONSTS)
            pe.wait_ge(s["ones_ready"], 1)
            def tokens(b, first):
                pe.wait_ge(s["xn_ready"], b + 1)
                if not first:
                    pe.wait_ge(s["q_sq"], b * HP - 1)
                for k in range(KC):
                    for t in range(NT):
                        last = pe.transpose(bQ[:, k * L + t * P:k * L + (t + 1) * P],
                                            xn[:, t, k * P:(k + 1) * P], ident[:, :])
                last.then_inc(s["xnT_mm"], 1)

            def key_values(b, which, first):
                for n in range(3):
                    if n == 0 and which == 0:
                        pe.wait_ge(s["ctx_copy"], b + 1)
                    if n == 0 and not first:
                        if which == 0:
                            pe.wait_ge(s["exp_done"], b * H)
                        else:
                            pe.wait_ge(s["q_sq"], b * HP)
                            pe.wait_ge(s["pt_lo"], b * 2 * HP)
                    if n == 1 and which == 0:
                        pe.wait_ge(s["xT_lo"], b + 1)
                    bank = [K_BANK, V_BANK][which][n]
                    w = 2 * (n > 0) + which
                    for k in range(KC):
                        if n == 0:
                            src = [ctxb[:, j, k, 0:1 + which, :].rearrange("p r n -> p (r n)") for j in range(2)]
                        else:
                            src = [xT[:, j, k, (n - 1) * P:n * P] for j in range(2)]
                        last = product(pe, bank[0:[ROWS, V_ROWS][which][n], :], src, [wkv[:, j, w, k, :] for j in range(2)],
                                       k == 0, k == KC - 1)
                    last.then_inc(s["kv_mm"], 1)

            def keys(b):
                for g in range(G):
                    if g == 0:
                        pe.wait_ge(s["kr_ready"], b * 3 + 3)
                    if g == 2:
                        pe.wait_ge(s["v_lo"], b * 3 + 3)
                    for n in (1, 0, 2):
                        last = pe.transpose(KT_BANK[g][:, COL[n]:COL[n] + ROWS[n]], kr[0:ROWS[n], n, g, :],
                                            ident[0:ROWS[n], 0:ROWS[n]])
                    last.then_inc(s["kT_mm"], 1)

            def batch(b, first, following):
                def project(i):
                    if i >= 2:
                        pe.wait_ge(s["q_sq"], b * HP + i - 1)
                    elif i == 1:
                        pe.wait_ge(s["v_lo"], b * 3 + 1)
                    else:
                        pe.wait_ge(s["kn_ready"], b * 3 + 3)
                    for hh in range(2):
                        h = 2 * i + hh
                        for k in range(KC):
                            last = product(pe, Q_BANK[i % 2][:, hh * L:(hh + 1) * L], [wq[:, j, k, h * D:(h + 1) * D] for j in range(2)],
                                           [xT[:, j, k, :] for j in range(2)], k == 0, k == KC - 1)
                    last.then_inc(s["q_mm"], 1)

                def scores(i):
                    pe.wait_ge(s["q_lo"], b * HP + i + 3)
                    if i == 0:
                        pe.wait_ge(s["kT_lo"], b * G + G)
                    g = i // 2
                    for hh in range(2):
                        if i:
                            pe.wait_ge(s["exp_done"], b * H + 2 * i - 1 + hh)
                        for t in range(NT):
                            o = bS[hh][:, AT[t]:AT[t] + SPAN[t]]
                            query = [qT[:, i % 2, j, hh, t * P:(t + 1) * P] for j in range(2)]
                            if t == 0:
                                product(pe, o[:, P:P + T], query, [kT[:, j, g, 0:T] for j in range(2)], True, True)
                                product(pe, o[:, 0:P], query, [kT[:, j, g, T:T + P] for j in range(2)], True, False)
                                diagonal = o[:, 0:P]
                            else:
                                product(pe, o, query, [kT[:, j, g, 0:SPAN[t]] for j in range(2)], True, False)
                                diagonal = o[:, L - P + T:L + T]
                            last = pe.matmul(diagonal, identb[:, :], maskb[:, :], start=False, stop=True,
                                             skip_group_check=True)
                        last.then_inc(s["s_mm"], 1)

                def sums(i):
                    pe.wait_ge(s["q_sq"], b * HP + i + 1)
                    if i == 0:
                        if not first:
                            pe.wait_ge(s["x_upd"], b * NT)
                    else:
                        pe.wait_ge(s["ssq_read"], b * HP + i)
                    if i >= 5:
                        pe.wait_ge(s["o_lo"], b * 2 * G + 2 * ((i - 5) // 2) + 2)
                    for hh in range(2):
                        for t in range(NT):
                            c = 2 * hh + t
                            last = pe.matmul(bM[:, c:c + 1], sq[:, hh * L + t * P:hh * L + (t + 1) * P], ones[:, :],
                                             start=True, stop=True, skip_group_check=True)
                    last.then_inc(s["ssq_mm"], 1)

                def transpose_probs(i):
                    pe.wait_ge(s["p_norm"], b * HP + i + 1)
                    pv = p[:, i % 2]
                    if i == 0:
                        pe.wait_ge(s["kT_lo"], b * G + G)
                    else:
                        pe.wait_ge(s["pt_lo"], b * 2 * HP + 2 * i)
                    for j, bank in enumerate((bPa, bPb)):
                        for k in range(2):
                            for hh in range(2):
                                c, at = (k * 2 + hh) * P, (2 * j + k) * P
                                last = pe.transpose(bank[:, c:c + P], pv[:, hh, at:at + P], ident[:, :])
                        last.then_inc(s["pt_mm"], 1)

                def attend(g):
                    pe.wait_ge(s["pt_lo"], b * 2 * HP + 4 * g + 4)
                    for t in range(NT):
                        if t == 0:
                            if g:
                                pe.wait_ge(s["o_lo"], b * 2 * G + 2 * g - 1)
                        else:
                            pe.wait_ge(s["ssq_read"], b * HP + min(2 * g + 5, HP))
                        o = [bV, bM][t][:, :]
                        if t == 0:
                            blocks = [(slice(0, P), 1, pta, 0), (slice(0, T), 0, pta, 1)]
                        else:
                            blocks = [(slice(T, P), 0, pta, 1), (slice(0, P), 1, ptb, 0), (slice(0, P), 2, ptb, 1)]
                        for m, (r, n, pt, k) in enumerate(blocks):
                            last = product(pe, o, [v[r, j, n, g * D:(g + 1) * D] for j in range(2)],
                                           [pt[r, g % 2, j, k].rearrange("p h n -> p (h n)") for j in range(2)],
                                           m == 0, m == len(blocks) - 1)
                        last.then_inc(s["pv_mm"], 1)

                for i in range(HP + 4):
                    if 0 <= i - 2 < HP:
                        scores(i - 2)
                    if 2 <= i <= HP:
                        sums(i - 1)
                    if i < HP:
                        project(i)
                    if i == 0:
                        keys(b)
                    if i == 1:
                        sums(0)
                    if 0 <= i - 3 < HP:
                        transpose_probs(i - 3)
                    if i == HP and following:
                        tokens(b + 1, False)
                    if i == HP + 2 and following:
                        key_values(b + 1, 0, False)
                    if i >= 5 and i % 2 == 1:
                        attend((i - 5) // 2)
                if following:
                    key_values(b + 1, 1, False)
                pe.wait_ge(s["stage_free"], 3)
                pe.wait_ge(s["o_lo"], b * 2 * G + 2 * G)
                for t in range(NT):
                    for h in range(H):
                        last = product(pe, [bV, bM][t][:, 0:DM], [oT[:, j, h, t * P:(t + 1) * P] for j in range(2)],
                                       [wo[:, j, h, :] for j in range(2)], h == 0, h == H - 1)
                    last.then_inc(s["wo_mm"], 1)

            tokens(0, True)
            pe.wait_ge(s["ctx_lo"], 1)
            pe.wait_ge(s["stage_free"], 1)
            key_values(0, 0, True)
            key_values(0, 1, True)
            pe.wait_ge(s["stage_free"], 2)
            batch(0, True, True)
            with pe.Fori(1, B - 1) as b:
                batch(b, False, True)
            batch(B - 1, False, False)
            if last_phase == 1:
                return

            pe.sem_inc(s["f_down"], 4)
            pe.wait_ge(s["gw_lo"], 1)
            pe.wait_ge(s["x_upd"], B * NT)

            def transpose_tokens(c, first):
                pe.wait_ge(s["fx_ready"], first + c + 1)
                for k in range(KC):
                    for t in range(TG):
                        last = pe.transpose([bQ, bM][k][:, t * P:(t + 1) * P], gxn[:, t, k * P:(k + 1) * P], ident[:, :])
                    last.then_inc(s["fx_mm"], 1)

            def down0(c, u):
                U = E0 * FC
                e, f = u // FC, u % FC
                pe.wait_ge(s["f_hlo"], c * U + u + 1)
                if f == 0 and e:
                    pe.wait_ge(s["f_upd"], c * TG * E0 + TG)
                for t in range(TG):
                    y = [bV, bR][t // 2][:, (t % 2) * DM:(t % 2 + 1) * DM]
                    last = product(pe, y, [hT[:, u % 4, j, t * P:(t + 1) * P] for j in range(2)],
                                   [wd0[:, j, e, f, :] for j in range(2)], f == 0 and t % 2 == 0, f == FC - 1)
                last.then_inc(s["f_down"], 1)

            def group0(c):
                transpose_tokens(c, 0)
                pe.wait_ge(s["fx_lo"], c * KC + KC)
                for t in range(TG):
                    for k in range(KC):
                        last = product(pe, bM[:, t * E0:(t + 1) * E0], [gxT[:, j, k, t * P:(t + 1) * P] for j in range(2)],
                                       [gw0p[:, j, k, :] for j in range(2)], k == 0, k == KC - 1)
                last.then_inc(s["f_logit"], 1)
                U = E0 * FC
                for u in range(U + 2):
                    if u < U:
                        e, f = u // FC, u % FC
                        pe.wait_ge(s["f_h"], c * U + u + 1)
                        for w, bank, done in ((wg0, bS[u % 2], "fg_mm"), (wu0, [bPa, bPb][u % 2], "fu_mm")):
                            if u == 0:
                                pe.wait_ge(s["fw_lo"], 1 if done == "fg_mm" else 3)
                            for k in range(KC):
                                last = product(pe, bank[:, :], [w[:, j, e, k, f * P:(f + 1) * P] for j in range(2)],
                                               [gxT[:, j, k, :] for j in range(2)], k == 0, k == KC - 1)
                            last.then_inc(s[done], 1)
                    if u >= 2:
                        down0(c, u - 2)

            with pe.Fori(0, NG) as c:
                group0(c)
            if last_phase == 2:
                return

            pe.wait_ge(s["a_wint"], 1)
            wqp = flat[:, L1_SPLIT:L1_ALL].rearrange("p (j o n) -> p j o n", j=2, o=KC)
            for j in range(2):
                for k in range(KC):
                    for o in range(KC):
                        last = pe.transpose([bS0, bS1][j][:, k * DM + o * P:k * DM + (o + 1) * P],
                                            wqp[:, j, o, k * P:(k + 1) * P], ident[:, :])
                last.then_inc(s["a_wT"], 1)
            for j in range(4):
                last = pe.matmul(bPa[:, j * P:(j + 1) * P], onesM[:, :], diag[:, j, :], start=True, stop=True,
                                 skip_group_check=True)
            last.then_inc(s["a_srow"], 1)
            pe.wait_ge(s["lw_lo"], 1)
            wkv1 = w1("kv", KC)
            for m in range(KC):
                for k in range(KC):
                    last = product(pe, [bPb, bR][m][:, :], [wkv1[j][:, k, m * P:(m + 1) * P] for j in range(2)],
                                   [ctxT[:, j, k, :] for j in range(2)], k == 0, k == KC - 1)
                last.then_inc(s["a_k"], 1)
            pe.wait_ge(s["a_klo"], 1)
            pe.wait_ge(s["a_srow_read"], 1)
            pe.wait_ge(s["a_wq"], 2)

            def batch1(b):
                pe.wait_ge(s["a_x"], b + 1)
                for k in range(KC):
                    for t in range(NT):
                        last = pe.transpose(bM[:, k * L + t * P:k * L + (t + 1) * P], xi[:, t, k * P:(k + 1) * P],
                                            ident[:, :])
                last.then_inc(s["a_xT"], 1)
                pe.wait_ge(s["a_ctx"], b + 1)
                for k in range(KC):
                    last = product(pe, bV[:, 0:DM], [ctxd[:, j, k].rearrange("p r n -> p (r n)") for j in range(2)],
                                   [wkv1[j][:, k, DM:2 * DM] for j in range(2)], k == 0, k == KC - 1)
                last.then_inc(s["a_v"], 1)
                pe.wait_ge(s["a_xq"], b + 1)
                for t in range(NT):
                    for k in range(KC):
                        last = pe.matmul(bQ[:, t * DM:(t + 1) * DM], xqT[:, k, t * P:(t + 1) * P], wint[:, 0, k, :],
                                         start=(k == 0), stop=(k == KC - 1), skip_group_check=True)
                last.then_inc(s["a_q"], 1)
                pe.wait_ge(s["a_q1"], b + 1)
                for k in range(KC):
                    for t in range(NT):
                        last = pe.transpose(bM[:, k * L + t * P:k * L + (t + 1) * P], q1[:, t, k * P:(k + 1) * P],
                                            ident[:, :])
                last.then_inc(s["a_q1T"], 1)
                pe.wait_ge(s["a_qlo"], b + 1)
                pe.wait_ge(s["a_kbd"], b + 1)
                for u in range(4):
                    t, k = u // 2, u % 2
                    product(pe, UNIT_S[u][:, :], [q1T[:, j, k, t * P:(t + 1) * P] for j in range(2)],
                            [kbd[:, j, k].rearrange("p h n -> p (h n)") for j in range(2)], True, True)\
                        .then_inc(s["a_s"], 1)

                def transpose_probs1(u):
                    pe.wait_ge(s["a_p"], 4 * b + u + 1)
                    if u >= 2:
                        pe.wait_ge(s["a_ptlo"], 4 * b + u - 1)
                    flat_e = e1[:, u].rearrange("p h n -> p (h n)")
                    for m in range(4):
                        last = pe.transpose([bR, bQ][u % 2][:, m * P:(m + 1) * P], flat_e[:, m * P:(m + 1) * P],
                                            ident[:, :])
                    last.then_inc(s["a_pt"], 1)

                def attend1(u):
                    t, k = u // 2, u % 2
                    pe.wait_ge(s["a_ptlo"], 4 * b + u + 1)
                    if u == 0:
                        pe.wait_ge(s["a_vlo"], b + 1)
                    for m in range(4):
                        c = k * P + m * 2 * D1
                        last = product(pe, [bV, bM][t][:, c:c + 2 * D1], [pt1[:, u, j, m, :] for j in range(2)],
                                       [vbd[:, j, c:c + 2 * D1] for j in range(2)], True, True)
                    if k == KC - 1:
                        last.then_inc(s["a_o"], 1)

                transpose_probs1(0)
                for u in range(1, 4):
                    transpose_probs1(u)
                    attend1(u - 1)
                attend1(3)
                pe.wait_ge(s["a_oi"], b + 1)
                for k in range(KC):
                    for t in range(NT):
                        last = pe.transpose(bR[:, k * L + t * P:k * L + (t + 1) * P], xi[:, t, k * P:(k + 1) * P],
                                            ident[:, :])
                last.then_inc(s["a_oT"], 1)
                pe.wait_ge(s["a_oq"], b + 1)
                for t in range(NT):
                    for k in range(KC):
                        last = pe.matmul(bQ[:, t * DM:(t + 1) * DM], xqT[:, k, t * P:(t + 1) * P], wint[:, 1, k, :],
                                         start=(k == 0), stop=(k == KC - 1), skip_group_check=True)
                last.then_inc(s["a_y"], 1)

            with pe.Fori(0, B) as b:
                batch1(b)
            if last_phase == 3:
                return

            wr, wg1, wu1, wd1 = w1("router", KC), w1("gate", KC), w1("up", KC), w1("down", 1)
            wsg, wsu, wsd = w1("sgate", KC), w1("sup", KC), w1("sdown", 2)
            pe.wait_ge(s["a_upd"], B)

            def group1(c):
                transpose_tokens(c, NG)
                pe.wait_ge(s["fx_lo"], NG * KC + c * KC + KC)
                for t in range(TG):
                    for k in range(KC):
                        last = product(pe, bR[:, t * E1:(t + 1) * E1], [gxT[:, j, k, t * P:(t + 1) * P] for j in range(2)],
                                       [wr[j][:, k, :] for j in range(2)], k == 0, k == KC - 1)
                last.then_inc(s["r_logit"], 1)

                def unit(u):
                    pe.wait_ge(s["m_h"], c * U1 + u + 1)
                    for ws, wb, bank, done in ((wsg, wg1, bS[u % 2], "m_g"), (wsu, wu1, [bPa, bPb][u % 2], "m_u")):
                        for k in range(KC):
                            tok = [gxT[:, j, k, :] for j in range(2)]
                            if u < 2:
                                last = product(pe, bank[:, :], [ws[j][:, k, u * P:(u + 1) * P] for j in range(2)], tok,
                                               k == 0, k == KC - 1)
                            else:
                                t, half = (u - 2) // 2, (u - 2) % 2
                                last = product(pe, bank[:, :], [a[:, t * P:(t + 1) * P] for a in tok],
                                               [wb[j][:, k, half * 512:(half + 1) * 512] for j in range(2)],
                                               k == 0, k == KC - 1)
                        last.then_inc(s[done], 1)

                unit(0)
                unit(1)
                pe.wait_ge(s["r_w"], c + 1)
                for t in range(TG):
                    last = pe.transpose(bR[:, t * P:(t + 1) * P], chosen[:, t, :], ident[:, :])
                last.then_inc(s["r_wT"], 1)
                pe.wait_ge(s["r_wTc"], c + 1)
                for t in range(TG):
                    last = pe.matmul(bM[:, t * KB:(t + 1) * KB], WT[:, t * P:(t + 1) * P], mixp[:, :], start=True,
                                     stop=True, skip_group_check=True)
                last.then_inc(s["r_c"], 1)
                for u in range(2, U1):
                    unit(u)
                pe.wait_ge(s["m_mixed"], c + 1)
                for t in range(TG):
                    last = pe.transpose(bQ[:, t * P:(t + 1) * P], mixed[:, t, :], ident[:, :])
                last.then_inc(s["m_mT"], 1)
                pe.wait_ge(s["m_mlo"], c + 1)
                for t in range(TG):
                    y = [bV, bM][t // 2][:, (t % 2) * DM:(t % 2 + 1) * DM]
                    tok = slice(t * P, (t + 1) * P)
                    product(pe, y, [mT[:, j, tok] for j in range(2)], [wd1[j][:, 0, :] for j in range(2)], True, False)
                    for f in range(2):
                        last = product(pe, y, [hT[:, f, j, tok] for j in range(2)], [wsd[j][:, f, :] for j in range(2)],
                                       False, f == 1)
                    if t % 2:
                        last.then_inc(s["m_y"], 1)

            with pe.Fori(0, NG) as c:
                group1(c)


def _rows(a, n):
    return a.reshape(n, 128, -1).transpose(1, 0, 2)


def _tables():
    inv = (np.float32(1.0) / np.float32(10000.0) ** (np.arange(0, D, 2, dtype=np.float32) / np.float32(D))).astype(np.float32)
    ang = np.outer(np.arange(L, dtype=np.float32), inv).astype(np.float32)
    ang = np.concatenate([ang, ang], -1)
    cos, sin = np.cos(ang).astype(np.float32), np.sin(ang).astype(np.float32)
    sin[:, :D // 2] *= -1
    return cos, sin


def kernel(**inputs):
    import concourse.bacc as _bacc
    import ml_dtypes
    from concourse.bass_utils import run_bass_kernel_spmd as _run

    a = {k: np.asarray(v) for k, v in inputs.items()}
    cos, sin = _tables()
    rot = np.concatenate([np.arange(D // 2, D), np.arange(0, D // 2)])
    qw, kw = a["L0_xattn_q_norm_w"], a["L0_xattn_k_norm_w"]
    f32 = np.float32
    arrays = {
        "x": _rows(a["x"].reshape(B * L, DM), B * NT),
        "ctxT": _rows(a["ctx_2048"].reshape(B * T, DM).T, KC),
        "gates": np.broadcast_to(np.concatenate([a["g_xattn"], a["g_ffn"]]), (P, 4)),
        "ident": np.eye(P, dtype=f32),
        "identb": np.eye(P).astype(ml_dtypes.bfloat16),
        "maskb": np.where(np.arange(P)[None, :] > np.arange(P)[:, None], MASKED, 0.0).astype(ml_dtypes.bfloat16),
        "cosT": cos.T, "sinT": sin.T,
        "cosR": _rows(cos, NT), "sinR": _rows(sin, NT),
        "qw": np.stack([qw, qw[rot]], 1),
        "kw": np.broadcast_to(np.stack([kw, kw[rot]]), (P, 2, D)),
        "w0_kv": np.stack([_rows(a["L0_xattn_" + n], KC) for n in ("wk_ctx", "wv_ctx", "wk", "wv")], 1).reshape(P, -1),
        "w0_q": _rows(a["L0_xattn_wq"], KC).reshape(P, -1),
        "w0_o": _rows(a["L0_xattn_wo"], H).reshape(P, -1),
        "w0_g": np.stack([_rows(w.T, KC) for w in a["L0_ffn_w_gate"]], 1).reshape(P, -1),
        "w0_u": np.stack([_rows(w.T, KC) for w in a["L0_ffn_w_up"]], 1).reshape(P, -1),
        "w0_d": np.stack([_rows(w.T, FC) for w in a["L0_ffn_w_down"]], 1).reshape(P, -1),
        "gw0": _rows(a["L0_ffn_gate_w"].T, KC),
        "w0_l1": np.concatenate([
            _rows(a[n].T if turned else a[n], k).reshape(P, -1)
            for n, k, turned in (("L1_xattn_wkv", KC, True), ("L1_ffn_w_router", KC, False), ("L1_ffn_w_gate", KC, False),
                                 ("L1_ffn_w_up", KC, False), ("L1_ffn_w_down", 1, False),
                                 ("L1_ffn_shared_w_gate", KC, False), ("L1_ffn_shared_w_up", KC, False),
                                 ("L1_ffn_shared_w_down", 2, False), ("L1_xattn_wq", KC, False),
                                 ("L1_xattn_wp", KC, False))], 1),
        "headmask": (np.arange(P)[:, None] // D1 == np.arange(HC)[None, :]).astype(f32),
        "keymask": (np.arange(P)[:, None] // T == np.arange(2)[None, :]).astype(f32),
        "rows1": np.broadcast_to(np.stack([a["L1_xattn_bq"], a["L1_xattn_bp"], a["L1_xattn_bkv"][DM:]]), (P, 3, DM)),
        "bk": a["L1_xattn_bkv"][:DM].reshape(KC, P).T,
        "iota": np.broadcast_to(np.arange(E1, dtype=f32), (P, E1)),
        "amp": a["L1_ffn_amplitudes"],
        "escale": a["L1_ffn_expert_scale"].reshape(P, 1),
    }
    arrays = {"in_" + k: np.ascontiguousarray(v) for k, v in arrays.items()}
    nc = _bacc.Bacc("TRN2", target_bir_lowering=False, num_devices=1)
    ap = {k[3:]: nc.dram_tensor(k, v.shape, mybir.dt.from_np(v.dtype), kind="ExternalInput").ap()
          for k, v in arrays.items()}
    out = nc.dram_tensor("out_0", (P, B * NT, DM), F32, kind="ExternalOutput").ap()
    flamingo_layers(nc, ap["x"], ap["ctxT"], ap["gates"], ap, {k: ap["w0_" + k] for k in ("kv", "q", "o", "g", "u", "d", "l1")}, out, LAST_PHASE)
    r = _run(nc, [arrays], core_ids=[0])
    return np.ascontiguousarray(r.results[0]["out_0"].transpose(1, 0, 2)).reshape(B, L, DM)
```

```python
from contextlib import ExitStack

import numpy as np

import concourse.bass as bass
from concourse import mybir

F32 = mybir.dt.float32
F16 = mybir.dt.float16
BF16 = mybir.dt.bfloat16
I32 = mybir.dt.int32
U32 = mybir.dt.uint32
ALU = mybir.AluOpType
ACT = mybir.ActivationFunctionType
AX = mybir.AxisListType

B, L, T, DM = 8, 256, 64, 256
P = 128
KC = DM // P
NT = L // P
H, G, D = 16, 4, 128
HP = H // 2
KEYS = T + L
E0, FF = 2, 1024

WS = 64.0
PS = 1024.0
MASKED = -1e30
LN_EPS = 1e-5
RMS_EPS = 1e-6
RSQRT_MAGIC = float(0x5F3759DF)
HS = 4.0
ROUND = 1.5 * 2.0 ** 23
TG = 4
NG = B * NT // TG
FC = FF // P
E1, KB, I1 = 128, 8, 128
H1, D1 = 16, 16
HC = P // D1
EPS1 = 1e-8


def rep(ap2, n):
    p, m = ap2.shape
    return ap2.unsqueeze(1).broadcast_to([p, n, m])


def spread(ap2, m):
    p, n = ap2.shape
    return ap2.unsqueeze(2).broadcast_to([p, n, m])


def flamingo_layers(nc, x_in, ctxT_in, gates_in, consts, w0, out):
    ctx = ExitStack()
    with ctx:
        def sb(name, shape, dt=F32):
            return ctx.enter_context(nc.sbuf_tensor(name, shape, dt))

        def sem(name):
            return ctx.enter_context(nc.semaphore(name))

        bQ, bS0, bS1, bR, bPa, bPb, bV, bM = (
            ctx.enter_context(nc.psum_tensor(n, [P, 512], F32))
            for n in ("bQ", "bS0", "bS1", "bR", "bPa", "bPb", "bV", "bM"))
        bS = [bS0, bS1]

        x = sb("x", [P, B * NT, DM])
        ctxT = sb("ctxT", [P, 2, KC, B * T], F16)
        ctxb = sb("ctxb", [P, 2, KC, 2, T], F16)
        ident = sb("ident", [P, P])
        identb = sb("identb", [P, P], BF16)
        maskb = sb("maskb", [P, P], BF16)
        ones = sb("ones", [P, 1])
        gates = sb("gates", [P, 4])
        tanhg = sb("tanhg", [P, 4])
        gscale = sb("gscale", [P, 4])
        cosT = sb("cosT", [P, L])
        sinT = sb("sinT", [P, L])
        cosR = sb("cosR", [P, NT, D])
        sinR = sb("sinR", [P, NT, D])
        qw = sb("qw", [P, 2])
        kw = sb("kw", [P, 2, D])
        gw0 = sb("gw0", [P, KC, E0])
        gw0p = sb("gw0p", [P, 2, KC, E0], F16)
        raw = sb("raw", [P, 3, 4096])
        parts = sb("parts", [P, 3, 2, 4096], F16)
        wkv = parts[:, 0].rearrange("p s (w k n) -> p s w k n", w=4, k=KC)
        wq = parts[:, 1].rearrange("p s (k n) -> p s k n", k=KC)
        wo = parts[:, 2].rearrange("p s (h n) -> p s h n", h=H)
        wg0 = parts[:, 0].rearrange("p s (e k n) -> p s e k n", e=E0, k=KC)
        wu0 = parts[:, 1].rearrange("p s (e k n) -> p s e k n", e=E0, k=KC)
        wd0 = parts[:, 2].rearrange("p s (e f n) -> p s e f n", e=E0, f=FC)
        flat = raw[:, :, :].rearrange("p a n -> p (a n)")
        flatp = parts[:, :, :, :].rearrange("p a s n -> p (a s n)")
        L1_COLS, n1 = {}, 0
        for name, width in (("kv", KC * 2 * DM), ("router", KC * E1), ("gate", KC * KB * I1), ("up", KC * KB * I1),
                            ("down", DM), ("sgate", KC * 2 * I1), ("sup", KC * 2 * I1), ("sdown", 2 * DM),
                            ("q", KC * DM), ("p", KC * DM)):
            L1_COLS[name] = (n1, width)
            n1 += width
        L1_ALL = n1
        L1_SPLIT = n1 - 2 * KC * DM

        L1_KV = L1_COLS["kv"][1]

        def w1(name, k):
            at_, width = L1_COLS[name]
            return [flatp[:, j * L1_SPLIT + at_:j * L1_SPLIT + at_ + width].rearrange("p (k n) -> p k n", k=k)
                    for j in range(2)]

        outer = ctx
        ctx = ExitStack()
        stats = sb("stats", [P, NT, 6])
        mv = sb("mv", [P, NT, 2])
        nt0 = sb("nt0", [P, 16])
        nt1 = sb("nt1", [P, 16])
        rstd = sb("rstd", [P, NT])
        xn = sb("xn", [P, NT, DM])
        xT = sb("xT", [P, 2, KC, L], F16)
        sqk = sb("sqk", [P, 512])
        ssk = sb("ssk", [P, 3 * G])
        rk = sb("rk", [P, 3 * G])
        kr = sb("kr", [P, 3, G, D])
        ctx32 = kr[:, :, :, :].rearrange("p n g d -> p (n g d)")[:, 0:KC * B * T].rearrange("p (k n) -> p k n", k=KC)
        kT = sb("kT", [P, 2, G, KEYS], F16)
        v = sb("v", [P, 2, 3, G * D], F16)
        sq = sb("sq", [P, 512])
        qa = sb("qa", [P, 2, 2, L])
        qs = sb("qs", [P, 2, 2, L])
        ks = qs[:, :, :, :].rearrange("p a b n -> p a (b n)").rearrange("p a (g d) -> p a g d", g=G)
        qT = sb("qT", [P, 2, 2, 2, L], F16)
        rv = sb("rv", [P, 3, 4 + NT])
        ra = sb("ra", [P, 4 + NT])
        rq = sb("rq", [P, 3, 4 + NT])
        negmax = sb("negmax", [P, 2, 4])
        ebias = sb("ebias", [P, 2, 4])
        esum = sb("esum", [P, 2, 4])
        einv = sb("einv", [P, 2, 4])
        p = sb("p", [P, 2, 2, 512])
        kn = p[:, :, :, :].rearrange("p a b n -> p (a b n)")[:, 0:3 * G * D].rearrange("p (n g d) -> p n g d", n=3, g=G)
        pta = sb("pta", [P, 2, 2, 2, 4, P], F16)
        ptb = sb("ptb", [P, 2, 2, 2, 4, P], F16)
        o32 = sb("o32", [P, NT, 4, P])
        oT = sb("oT", [P, 2, H, L], F16)
        ctx.close()
        ctx = outer

        gstats = sb("gstats", [P, TG, 6])
        gmv = sb("gmv", [P, TG, 2])
        gvar = sb("gvar", [P, TG])
        grstd = sb("grstd", [P, TG])
        gnt = sb("gnt", [P, 2, 8])
        gxn = sb("gxn", [P, TG, DM])
        gxT = sb("gxT", [P, 2, KC, TG * P], F16)
        lg = sb("lg", [P, TG, E0])
        ld = sb("ld", [P, TG])
        la = sb("la", [P, TG])
        lt = sb("lt", [P, TG])
        topw = sb("topw", [P, TG])
        cf = sb("cf", [P, E0, TG])
        cfg = sb("cfg", [P, E0, TG])
        sg = sb("sg", [P, 2, TG * P])
        hh32 = sb("hh32", [P, 2, TG * P])
        hT = sb("hT", [P, 4, 2, TG * P], F16)
        headmask = sb("headmask", [P, HC])
        keymask = sb("keymask", [P, 2])
        rows1 = sb("rows1", [P, 3, DM])
        bk = sb("bk", [P, KC])
        iota = sb("iota", [P, E1])
        onesM = sb("onesM", [P, P])
        wabs = sb("wabs", [P, 4])
        wsc = sb("wsc", [P, 4])
        winv = sb("winv", [P, 4])
        diag = sb("diag", [P, 4, P])
        srow = sb("srow", [P, 2, DM])
        wint = sb("wint", [P, 2, KC, DM], F16)
        k1 = sb("k1", [P, KC, B * T])
        k1p = sb("k1p", [P, 2, KC, B * T], F16)
        kbd = sb("kbd", [P, 2, KC, HC, T], F16)
        ctxd = sb("ctxd", [P, 2, KC, 2, T], F16)
        v1 = sb("v1", [P, DM])
        vbd = sb("vbd", [P, 2, DM], F16)
        xabs = sb("xabs", [P, NT])
        xs = sb("xs", [P, NT])
        xsi = sb("xsi", [P, NT])
        xi = sb("xi", [P, NT, DM])
        xqT = sb("xqT", [P, KC, L], F16)
        q1 = sb("q1", [P, NT, DM])
        q1T = sb("q1T", [P, 2, KC, L], F16)
        mx1 = sb("mx1", [P, 4, HC])
        e1 = sb("e1", [P, 4, HC, T])
        es1 = sb("es1", [P, 4, HC])
        ei1 = sb("ei1", [P, 4, HC])
        pt1 = sb("pt1", [P, 4, 2, 4, P], F16)
        oabs = sb("oabs", [P, NT])
        os1 = sb("os1", [P, NT])
        osi = sb("osi", [P, NT])
        oi = sg[:, 0, :].rearrange("p (t n) -> p t n", t=NT)
        y1 = sg[:, 1, :].rearrange("p (t n) -> p t n", t=NT)
        oqT = gxT[:, 0, :, 0:L]
        amp = sb("amp", [P, KB, 2])
        mixp = sb("mixp", [P, KB])
        mixs = sb("mixs", [P, 2])
        escale = sb("escale", [P, 1])
        rmx = sb("rmx", [P, TG])
        rex = sb("rex", [P, TG, E1])
        rsum = sb("rsum", [P, TG])
        rinv = sb("rinv", [P, TG])
        top8 = sb("top8", [P, TG, 8])
        idx8 = sb("idx8", [P, TG, 8], U32)
        idxf = sb("idxf", [P, TG, 8])
        tw = sb("tw", [P, TG])
        chosen = sb("chosen", [P, TG, E1])
        WT = sb("WT", [P, TG * P])
        cc = sb("cc", [P, TG, KB])
        mixed = sb("mixed", [P, TG, I1])
        mT = sb("mT", [P, 2, TG * P], F16)

        names = """x_in x_rest_in ctx_in const_in w_in0 w_in1 w_in2 gw_hi gw_lo w_hi stage_free ctx_hi ctx_lo ones_ready
            gate_tanh xn_ready xnT_mm xT_hi xT_lo kv_mm k_sq k_ssq kn_ready kr_ready kT_mm kT_hi kT_lo v_hi v_lo
            q_mm q_sq q_rope q_hi q_lo ssq_mm s_mm bias_ready ssq_read ctx_copy exp_done inv_ready p_norm pt_mm
            pt_hi pt_lo pv_mm o_hi o_lo wo_mm x_upd dve_step pool_step stored pool_held l1_in c1_in lw_hi lw_lo
            lr_hi lr_lo a_wint a_wT a_wq a_srow a_srow_read a_k a_k1 a_khi a_klo a_x a_xT a_xq a_q a_q1 a_q1T a_qhi
            a_qlo a_kbd a_ctx a_v a_v1 a_vhi a_vlo a_s a_e a_exp a_inv a_p a_pt a_pthi a_ptlo a_o a_oi a_oT a_oq a_y
            a_upd r_logit r_e r_exp r_w r_wT r_wTc r_c r_cc m_g m_u m_silu m_h m_hi m_lo m_mixed m_mT m_mhi m_mlo
            m_y m_upd fw_hi fw_lo fx_ready fx_mm fx_hi fx_lo f_logit f_absd f_tanh fg_mm fu_mm f_silu f_h f_hhi
            f_hlo f_down f_upd kc_mul ks_mul""".split()
        s = {n: sem(n) for n in names}

        block = ctx.enter_context(nc.Block())

        def product(pe, out_ap, lhsT, rhs, first, last):
            pe.matmul(out_ap, lhsT[0], rhs[0], start=first, stop=False, skip_group_check=True)
            pe.matmul(out_ap, lhsT[0], rhs[1], start=False, stop=False, skip_group_check=True)
            return pe.matmul(out_ap, lhsT[1], rhs[0], start=False, stop=last, skip_group_check=True)

        ROWS = [T, P, P]
        K_BANK = [bS0, bS1, bQ]
        V_BANK = [bR, bPa, bPb]
        V_ROWS = [2 * T, P, P]
        Q_BANK = [bQ, bR]
        TILES = [1, 0]
        COL = [0, T, T + P]
        KT_BANK = [bS0, bS1, bPa, bPb]
        SPAN = [T + P, T + L]
        AT = [0, T + P]


        @block.sync
        def _(sp):
            sp.dma_start(x[:, 0:NT, :], x_in[:, 0:NT, :]).then_inc(s["x_in"], 16)
            sp.dma_start(ctx32[:, :, :], ctxT_in).then_inc(s["ctx_in"], 16)
            sp.dma_start(raw[:, 0, :], w0["kv"]).then_inc(s["w_in0"], 16)
            for dst, name in ((ident, "ident"), (identb, "identb"), (maskb, "maskb"), (cosT, "cosT"), (sinT, "sinT"),
                              (cosR, "cosR"), (sinR, "sinR"), (qw, "qw"), (kw, "kw"), (gw0, "gw0")):
                sp.dma_start(dst[:], consts[name]).then_inc(s["const_in"], 16)
            sp.dma_start(gates[:, :], gates_in).then_inc(s["const_in"], 16)
            sp.dma_start(raw[:, 1, :], w0["q"]).then_inc(s["w_in1"], 16)
            sp.dma_start(raw[:, 2, :], w0["o"]).then_inc(s["w_in2"], 16)
            sp.dma_start(x[:, NT:B * NT, :], x_in[:, NT:B * NT, :]).then_inc(s["x_rest_in"], 16)
            for n, name in enumerate(("g", "u", "d")):
                sp.wait_ge(s["stage_free"], n + 1)
                sp.dma_start(raw[:, n, :], w0[name]).then_inc(s[f"w_in{n}"], 16)
            sp.wait_ge(s["x_upd"], NT * B)
            for dst, name in ((headmask, "headmask"), (keymask, "keymask"), (rows1, "rows1"), (bk, "bk"),
                              (iota, "iota"), (amp, "amp"), (escale, "escale")):
                sp.dma_start(dst[:], consts[name]).then_inc(s["c1_in"], 16)
            sp.wait_ge(s["fw_lo"], 3)
            sp.dma_start(flat[:, 0:L1_ALL], w0["l1"]).then_inc(s["l1_in"], 16)
            for c in range(NG):
                sp.wait_ge(s["m_upd"], (c + 1) * TG + 1)
                sp.dma_start(out[:, c * TG:(c + 1) * TG, :], x[:, c * TG:(c + 1) * TG, :]).then_inc(s["stored"], 16)
            sp.wait_ge(s["stored"], 16 * NG)

        CONSTS = 11
        CONSTS1 = 7
        UNIT_S = [bS0, bS1, bPa, bPb]
        TOKENS_0 = [bQ, bM]
        TOKENS_1 = [bQ, bR]
        U1 = 10

        @block.scalar
        def _(act):
            def split_hi(n):
                act.wait_ge(s[f"w_in{n}"], 16)
                act.activation(parts[:, n, 0, :], raw[:, n, :], ACT.Copy, scale=WS).then_inc(s["w_hi"], 1)

            def tokens(b):
                act.wait_ge(s["xnT_mm"], b + 1)
                act.wait_ge(s["q_mm"], b * HP + 1)
                act.activation(xT[:, 0], bQ[:, :].rearrange("p (k n) -> p k n", k=KC), ACT.Copy)\
                   .then_inc(s["xT_hi"], 1)

            def context(b):
                for half in range(2):
                    last = act.activation(ctxb[:, :, :, half, :], ctxT[:, :, :, bass.ds(b * T, T)], ACT.Copy)
                last.then_inc(s["ctx_copy"], 1)

            def key_squares(b):
                for n in range(3):
                    act.wait_ge(s["kv_mm"], b * 6 + n + 1)
                    if n:
                        act.wait_ge(s["k_ssq"], b * 3 + n)
                    act.activation(sqk[0:ROWS[n], :], K_BANK[n][0:ROWS[n], :], ACT.Square)\
                       .then_inc(s["k_sq"], 1)

            def values(b):
                for n in range(3):
                    act.wait_ge(s["kv_mm"], b * 6 + 3 + n + 1)
                    act.activation(v[0:V_ROWS[n], 0, n, :], V_BANK[n][0:V_ROWS[n], :], ACT.Copy)\
                       .then_inc(s["v_hi"], 1)

            def keys(b):
                for g in range(G):
                    act.wait_ge(s["kT_mm"], b * G + g + 1)
                    act.activation(kT[:, 0, g, :], KT_BANK[g][:, 0:KEYS], ACT.Copy).then_inc(s["kT_hi"], 1)

            def batch(b, following):
                def square(i):
                    act.wait_ge(s["q_rope"], b * HP + i + 1)
                    act.wait_ge(s["ssq_mm"], b * HP + i + 1)
                    act.activation(sq[:, :], Q_BANK[i % 2][:, :], ACT.Square).then_inc(s["q_sq"], 1)

                def exps(i):
                    act.wait_ge(s["pt_mm"], b * 2 * HP + 2 * i + 2)
                    for hh in range(2):
                        act.wait_ge(s["bias_ready"], b * H + 2 * i + hh + 1)
                        for t in range(NT):
                            j = 2 * hh + t
                            last = act.activation(
                                p[:, i % 2, hh, AT[t]:AT[t] + SPAN[t]], bS[hh][:, AT[t]:AT[t] + SPAN[t]], ACT.Exp,
                                bias=ebias[:, i % 2, j:j + 1], scale=rq[:, i % 3, j:j + 1],
                                accum_out=esum[:, i % 2, j:j + 1])
                        last.then_inc(s["exp_done"], 1)

                def probs_hi(i):
                    g, two = i // 2, slice(2 * (i % 2), 2 * (i % 2) + 2)
                    act.wait_ge(s["pv_mm"], b * 2 * G + 2 * g + 2)
                    for j, (dst, bank) in enumerate(((pta, bPa), (ptb, bPb))):
                        act.wait_ge(s["pt_mm"], b * 2 * HP + 2 * i + 4 + j + 1)
                        act.activation(dst[:, g % 2, 0, :, two, :],
                                       bank[:, :].rearrange("p (k h n) -> p k h n", k=2, h=2), ACT.Copy)\
                           .then_inc(s["pt_hi"], 1)

                def out_hi(g):
                    for n, t in enumerate(TILES):
                        act.wait_ge(s["pv_mm"], b * 2 * G + 2 * g + 4 + n + 1)
                        bank = [bV, bM][t][:, :].rearrange("p (h n) -> p h n", h=4)
                        act.activation(oT[:, 0, 4 * g:4 * g + 4, t * P:(t + 1) * P], bank, ACT.Copy, scale=1.0 / PS)
                        act.wait_ge(s["o_lo"], b * 2 * G + 2 * g + n + 1)
                        act.activation(o32[:, t], bank, ACT.Copy, scale=1.0 / PS).then_inc(s["o_hi"], 1)

                for i in range(HP + 4):
                    if 0 <= i - 2 < HP:
                        exps(i - 2)
                    if 0 <= i - 3 < HP:
                        probs_hi(i - 3)
                    if i < HP:
                        square(i)
                    if i == 0:
                        keys(b)
                    if i == HP - 2 and following:
                        context(b + 1)
                    if i == HP and following:
                        tokens(b + 1)
                    if i == HP + 2 and following:
                        key_squares(b + 1)
                    if i >= 5 and i % 2 == 1:
                        out_hi((i - 5) // 2)
                if following:
                    values(b + 1)

            act.wait_ge(s["ctx_in"], 16)
            act.activation(ctxT[:, 0], ctx32[:, :, :], ACT.Copy).then_inc(s["ctx_hi"], 1)
            split_hi(0)
            act.wait_ge(s["ctx_lo"], 1)
            context(0)
            tokens(0)
            key_squares(0)
            values(0)
            split_hi(1)
            split_hi(2)
            act.wait_ge(s["const_in"], 16 * CONSTS)
            act.activation(tanhg[:, :], gates[:, :], ACT.Tanh).then_inc(s["gate_tanh"], 1)
            act.activation(gw0p[:, 0], gw0[:, :, :], ACT.Copy, scale=WS).then_inc(s["gw_hi"], 1)
            with act.Fori(0, B - 1) as b:
                batch(b, True)
            batch(B - 1, False)

            def ffn_split_hi(n):
                act.wait_ge(s[f"w_in{n}"], 32)
                act.activation(parts[:, n, 0, :], raw[:, n, :], ACT.Copy, scale=WS).then_inc(s["fw_hi"], 1)

            ffn_split_hi(0)
            ffn_split_hi(1)

            def tokens_hi(c, first, banks):
                for k in range(KC):
                    act.wait_ge(s["fx_mm"], first + c * KC + k + 1)
                    act.activation(gxT[:, 0, k], banks[k][:, :], ACT.Copy).then_inc(s["fx_hi"], 1)

            def group0(c, following):
                act.wait_ge(s["f_absd"], c + 1)
                act.activation(lt[:, :], la[:, :], ACT.Tanh, scale=0.5).then_inc(s["f_tanh"], 1)
                U = E0 * FC
                for u in range(U + 1):
                    if u < U:
                        act.wait_ge(s["fg_mm"], c * U + u + 1)
                        act.wait_ge(s["f_h"], c * U + u + 1)
                        act.activation(sg[:, u % 2, :], bS[u % 2][:, :], ACT.Silu, scale=1.0 / WS)\
                           .then_inc(s["f_silu"], 1)
                    if u >= 1:
                        act.wait_ge(s["f_h"], c * U + u - 1 + 3)
                        act.wait_ge(s["f_down"], c * U + u - 1 + 1)
                        act.activation(hT[:, (u - 1) % 4, 0, :], hh32[:, (u - 1) % 2, :], ACT.Copy)\
                           .then_inc(s["f_hhi"], 1)
                if following:
                    act.wait_ge(s["fu_mm"], c * U + U)
                    tokens_hi(c + 1, 0, TOKENS_0)

            tokens_hi(0, 0, TOKENS_0)
            act.wait_ge(s["wo_mm"], B * NT)
            ffn_split_hi(2)
            with act.Fori(0, NG - 1) as c:
                group0(c, True)
            group0(NG - 1, False)

            act.wait_ge(s["l1_in"], 16)
            act.activation(flatp[:, 0:L1_KV], flat[:, 0:L1_KV], ACT.Copy, scale=WS).then_inc(s["lw_hi"], 1)
            act.wait_ge(s["a_k1"], KC)
            act.activation(k1p[:, 0], k1[:, :, :], ACT.Copy).then_inc(s["a_khi"], 1)

            def values1(b, first):
                act.wait_ge(s["a_v1"], b + 1)
                if not first:
                    act.wait_ge(s["a_o"], NT * b)
                act.activation(vbd[:, 0, :], v1[:, :], ACT.Copy).then_inc(s["a_vhi"], 1)

            def queries1(b):
                act.wait_ge(s["a_q1T"], b + 1)
                act.activation(q1T[:, 0], bV[:, :].rearrange("p (k n) -> p k n", k=KC), ACT.Copy)\
                   .then_inc(s["a_qhi"], 1)

            def batch1(b, following):
                for u in range(4):
                    act.wait_ge(s["a_e"], 4 * b + u + 1)
                    for h in range(HC):
                        last = act.activation(e1[:, u, h, :], UNIT_S[u][:, h * T:(h + 1) * T], ACT.Exp,
                                              bias=mx1[:, u, h:h + 1], scale=float(D1) ** -0.5,
                                              accum_out=es1[:, u, h:h + 1])
                    last.then_inc(s["a_exp"], 1)
                for u in range(4):
                    act.wait_ge(s["a_pt"], 4 * b + u + 1)
                    act.activation(pt1[:, u, 0], [bR, bQ][u % 2][:, :].rearrange("p (m n) -> p m n", m=4), ACT.Copy)\
                       .then_inc(s["a_pthi"], 1)
                if following:
                    queries1(b + 1)
                    values1(b + 1, False)

            values1(0, True)
            queries1(0)
            act.activation(flatp[:, L1_KV:L1_SPLIT], flat[:, L1_KV:L1_SPLIT], ACT.Copy, scale=WS).then_inc(s["lr_hi"], 1)
            with act.Fori(0, B - 1) as b:
                batch1(b, True)
            batch1(B - 1, False)

            def gate1(c, u):
                act.wait_ge(s["m_g"], c * U1 + u + 1)
                act.wait_ge(s["m_h"], c * U1 + u + 1)
                act.activation(sg[:, u % 2, :], bS[u % 2][:, :], ACT.Silu, scale=1.0 / WS).then_inc(s["m_silu"], 1)

            def mixed_hi(c):
                act.wait_ge(s["m_mT"], c + 1)
                act.activation(mT[:, 0], bQ[:, :], ACT.Copy).then_inc(s["m_mhi"], 1)

            def front1(c, first):
                tokens_hi(c, NG * KC, TOKENS_1)
                if not first:
                    mixed_hi(c - 1)
                act.wait_ge(s["r_e"], c + 1)
                act.activation(rex[:, :, :], rex[:, :, :], ACT.Exp, scale=1.0 / WS).then_inc(s["r_exp"], 1)
                for u in range(2):
                    gate1(c, u)
                    act.wait_ge(s["m_h"], c * U1 + u + 3)
                    act.activation(hT[:, u, 0, :], hh32[:, u % 2, :], ACT.Copy).then_inc(s["m_hi"], 1)

            def group1(c, following):
                for u in range(2, U1):
                    gate1(c, u)
                if following:
                    act.wait_ge(s["m_u"], c * U1 + U1)
                    front1(c + 1, False)

            front1(0, True)
            with act.Fori(0, NG - 1) as c:
                group1(c, True)
            group1(NG - 1, False)
            mixed_hi(NG - 1)

        @block.vector
        def _(dve):
            count = [0]

            def mark(ins):
                count[0] += 1
                ins.then_inc(s["dve_step"], 1)
                return count[0]

            def step(ins):
                dve.wait_ge(s["dve_step"], mark(ins))

            def restart():
                dve.sem_clear(s["dve_step"])
                count[0] = 0

            def rsqrt(y, val, n, work=None):
                a = nt0[:, 0:n] if work is None else work
                step(dve.tensor_scalar(y.bitcast(I32), val.bitcast(I32), -0.5, RSQRT_MAGIC, ALU.mult, ALU.add))
                for _ in range(3):
                    step(dve.scalar_tensor_tensor(out=a, in0=y, scalar=-0.5, in1=val, op0=ALU.mult, op1=ALU.mult))
                    step(dve.tensor_tensor(a, a, y, ALU.mult))
                    step(dve.scalar_tensor_tensor(out=y, in0=a, scalar=1.5, in1=y, op0=ALU.add, op1=ALU.mult))

            def split_lo(n):
                dve.wait_ge(s["w_hi"], n + 1)
                dve.scalar_tensor_tensor(out=parts[:, n, 1, :], in0=raw[:, n, :], scalar=WS, in1=parts[:, n, 0, :],
                                         op0=ALU.mult, op1=ALU.subtract).then_inc(s["stage_free"], 1)

            def group_stats(c):
                for t in range(TG):
                    last = dve.bn_stats(gstats[:, t, :], x[:, c * TG + t, :])
                step(last)
                for t in range(TG):
                    last = dve.bn_aggr(gmv[:, t, :], gstats[:, t, :])
                step(last)
                step(dve.tensor_scalar(gvar[:, :], gmv[:, :, 1], LN_EPS, None, ALU.add))

            group_done = {"n": 0, "count": 0}

            def group_newton(upto):
                y, val, work = grstd[:, :], gvar[:, :], gnt[:, 0, 0:TG]
                for n in range(group_done["n"], min(upto, 10)):
                    if n:
                        dve.wait_ge(s["dve_step"], group_done["count"])
                    if n == 0:
                        ins = dve.tensor_scalar(y.bitcast(I32), val.bitcast(I32), -0.5, RSQRT_MAGIC, ALU.mult, ALU.add)
                    elif n % 3 == 1:
                        ins = dve.scalar_tensor_tensor(out=work, in0=y, scalar=-0.5, in1=val, op0=ALU.mult, op1=ALU.mult)
                    elif n % 3 == 2:
                        ins = dve.tensor_tensor(work, work, y, ALU.mult)
                    else:
                        ins = dve.scalar_tensor_tensor(out=y, in0=work, scalar=1.5, in1=y, op0=ALU.add, op1=ALU.mult)
                    group_done["n"], group_done["count"] = n + 1, mark(ins)

            def group_norms():
                rsqrt(grstd[:, :], gvar[:, :], TG, work=gnt[:, 0, 0:TG])

            def group_scales(c):
                for t in range(TG):
                    last = dve.tensor_scalar(gxn[:, t, :], x[:, c * TG + t, :], gmv[:, t, 0:1], grstd[:, t:t + 1],
                                             ALU.subtract, ALU.mult)
                last.then_inc(s["fx_ready"], 1)

            def ffn_split_lo(n):
                dve.wait_ge(s["fw_hi"], n + 1)
                dve.scalar_tensor_tensor(out=parts[:, n, 1, :], in0=raw[:, n, :], scalar=WS, in1=parts[:, n, 0, :],
                                         op0=ALU.mult, op1=ALU.subtract).then_inc(s["fw_lo"], 1)

            def norm_stats(b, val):
                for t in range(NT):
                    last = dve.bn_stats(stats[:, t, :], x[:, b * NT + t, :])
                step(last)
                for t in range(NT):
                    last = dve.bn_aggr(mv[:, t, :], stats[:, t, :])
                step(last)
                step(dve.tensor_scalar(val, mv[:, :, 1], LN_EPS, None, ALU.add))

            def norm_tokens(b, rstd):
                for t in range(NT):
                    last = dve.tensor_scalar(xn[:, t, :], x[:, b * NT + t, :], mv[:, t, 0:1], rstd[:, t:t + 1],
                                             ALU.subtract, ALU.mult)
                last.then_inc(s["xn_ready"], 1)

            def tokens(b):
                dve.wait_ge(s["xT_hi"], b + 1)
                dve.tensor_tensor(xT[:, 1], bQ[:, :].rearrange("p (k n) -> p k n", k=KC), xT[:, 0], ALU.subtract)\
                   .then_inc(s["xT_lo"], 1)

            def key_norms(b):
                for n in range(3):
                    dve.wait_ge(s["k_sq"], b * 3 + n + 1)
                    dve.tensor_reduce(ssk[0:ROWS[n], n * G:(n + 1) * G],
                                      sqk[0:ROWS[n], :].rearrange("p (g d) -> p g d", g=G), AX.X, ALU.add)\
                       .then_inc(s["k_ssq"], 1)
                dve.wait_ge(s["k_ssq"], b * 3 + 3)
                step(dve.tensor_scalar(nt1[:, 0:3 * G], ssk[:, :], 1.0 / D, WS * WS * RMS_EPS, ALU.mult, ALU.add))
                rsqrt(rk[:, :], nt1[:, 0:3 * G], 3 * G)

            def scale_keys(b):
                for n in range(3):
                    r = ROWS[n]
                    dve.tensor_tensor(kn[0:r, n], K_BANK[n][0:r, :].rearrange("p (g d) -> p g d", g=G),
                                      spread(rk[0:r, n * G:(n + 1) * G], D), ALU.mult).then_inc(s["kn_ready"], 1)
                for n in range(1, 3):
                    dve.wait_ge(s["kn_ready"], b * 3 + n + 1)
                    for lo_, hi_ in ((0, D // 2), (D // 2, 0)):
                        last = dve.tensor_tensor(ks[:, n - 1, :, lo_:lo_ + D // 2], kn[:, n, :, hi_:hi_ + D // 2],
                                                 rep(sinR[:, n - 1, lo_:lo_ + D // 2], G), ALU.mult)
                    last.then_inc(s["ks_mul"], 1)

            def values(b):
                for n in range(3):
                    dve.wait_ge(s["v_hi"], b * 3 + n + 1)
                    dve.tensor_tensor(v[0:V_ROWS[n], 1, n, :], V_BANK[n][0:V_ROWS[n], :], v[0:V_ROWS[n], 0, n, :],
                                      ALU.subtract).then_inc(s["v_lo"], 1)

            def keys(b):
                for g in range(G):
                    dve.wait_ge(s["kT_hi"], b * G + g + 1)
                    dve.tensor_tensor(kT[:, 1, g, :], KT_BANK[g][:, 0:KEYS], kT[:, 0, g, :], ALU.subtract)\
                       .then_inc(s["kT_lo"], 1)

            def batch(b, following):
                done, stepped = {}, {}

                def newton(i, upto):
                    y, val = rq[:, i % 3, :], rv[:, i % 3, :]
                    for n in range(done[i], upto):
                        dve.wait_ge(s["dve_step"], stepped[i])
                        if n % 3 == 0:
                            ins = dve.scalar_tensor_tensor(out=ra[:, :], in0=y, scalar=-0.5, in1=val, op0=ALU.mult,
                                                           op1=ALU.mult)
                        elif n % 3 == 1:
                            ins = dve.tensor_tensor(ra[:, :], ra[:, :], y, ALU.mult)
                        else:
                            ins = dve.scalar_tensor_tensor(out=y, in0=ra[:, :], scalar=1.5, in1=y, op0=ALU.add,
                                                           op1=ALU.mult)
                        stepped[i] = mark(ins)
                    done[i] = max(done[i], upto)

                def rope(i):
                    q = Q_BANK[i % 2][:, :].rearrange("p (h n) -> p h n", h=2)
                    dve.wait_ge(s["q_mm"], b * HP + i + 2)
                    dve.wait_ge(s["q_lo"], b * HP + i + 1)
                    if i == 0:
                        dve.wait_ge(s["kr_ready"], b * 3 + 3)
                    half = D // 2
                    dve.tensor_tensor(qa[:, i % 2], q, rep(cosT[:, :], 2), ALU.mult)
                    if i:
                        newton(i - 1, 2)
                    dve.tensor_tensor(qs[0:half, i % 2], q[half:D], rep(sinT[0:half, :], 2), ALU.mult)
                    if i:
                        newton(i - 1, 3)
                    dve.tensor_tensor(qs[half:D, i % 2], q[0:half], rep(sinT[half:D, :], 2), ALU.mult)\
                       .then_inc(s["q_rope"], 1)

                def max_bias(i):
                    for hh in range(2):
                        dve.wait_ge(s["s_mm"], b * H + 2 * i + hh + 1)
                        for t in range(NT):
                            j = 2 * hh + t
                            newton(i, 8 + t)
                            last = dve.tensor_reduce(negmax[:, i % 2, j:j + 1],
                                                     bS[hh][:, AT[t]:AT[t] + SPAN[t]], AX.X, ALU.max, negate=True)
                        before = mark(last)
                        newton(i, 9)
                        dve.wait_ge(s["dve_step"], max(before, stepped[i]))
                        two = slice(2 * hh, 2 * hh + 2)
                        dve.tensor_tensor(ebias[:, i % 2, two], negmax[:, i % 2, two], rq[:, i % 3, two], ALU.mult)\
                           .then_inc(s["bias_ready"], 1)

                def norms(i):
                    dve.wait_ge(s["ssq_mm"], b * HP + i + 2)
                    dve.tensor_scalar(rv[:, i % 3, 0:4], bM[:, 0:4], D * WS * WS * RMS_EPS, None, ALU.add)\
                       .then_inc(s["ssq_read"], 1)
                    dve.wait_ge(s["ssq_read"], b * HP + i + 1)
                    stepped[i] = mark(dve.tensor_scalar(rq[:, i % 3, :].bitcast(I32), rv[:, i % 3, :].bitcast(I32), -0.5,
                                                        RSQRT_MAGIC, ALU.mult, ALU.add))
                    done[i] = 0

                def inverse(i):
                    dve.wait_ge(s["exp_done"], b * H + 2 * i + 2)
                    dve.reciprocal(einv[:, i % 2, :], esum[:, i % 2, :]).then_inc(s["inv_ready"], 1)

                def probs_lo(i):
                    g, two = i // 2, slice(2 * (i % 2), 2 * (i % 2) + 2)
                    for j, (dst, bank) in enumerate(((pta, bPa), (ptb, bPb))):
                        if j and i + 2 < HP:
                            newton(i + 2, 6)
                        dve.wait_ge(s["pt_hi"], b * 2 * HP + 2 * i + j + 1)
                        dve.tensor_tensor(dst[:, g % 2, 1, :, two, :],
                                          bank[:, :].rearrange("p (k h n) -> p k h n", k=2, h=2),
                                          dst[:, g % 2, 0, :, two, :], ALU.subtract).then_inc(s["pt_lo"], 1)

                for i in range(HP + 4):
                    if 0 <= i - 2 < HP:
                        max_bias(i - 2)
                    if 1 <= i <= HP:
                        norms(i - 1)
                        newton(i - 1, 1)
                    if i < HP:
                        rope(i)
                    if i == 0:
                        keys(b)
                    if 1 <= i <= HP:
                        newton(i - 1, 4)
                    if 0 <= i - 2 < HP:
                        inverse(i - 2)
                    if 1 <= i <= HP:
                        newton(i - 1, 5)
                    if 0 <= i - 3 < HP:
                        probs_lo(i - 3)
                    if 1 <= i <= HP:
                        newton(i - 1, 7)
                    if following:
                        if i == 2:
                            norm_stats(b + 1, rv[:, 0, 4:4 + NT])
                        if i == 5:
                            norm_tokens(b + 1, rq[:, 0, 4:4 + NT])
                    if i == HP and following:
                        tokens(b + 1)
                    if i == HP + 2 and following:
                        key_norms(b + 1)
                if following:
                    scale_keys(b + 1)
                    values(b + 1)
                if not following:
                    dve.wait_ge(s["q_mm"], B * HP + 1)
                    dve.wait_ge(s["x_upd"], TG)
                    group_stats(0)
                    group_norms()
                    group_scales(0)
                    ffn_split_lo(0)
                for t in range(NT):
                    dve.wait_ge(s["wo_mm"], b * NT + t + 1)
                    dve.scalar_tensor_tensor(out=x[:, b * NT + t, :], in0=[bV, bM][t][:, 0:DM],
                                             scalar=gscale[:, 0:1], in1=x[:, b * NT + t, :],
                                             op0=ALU.mult, op1=ALU.add).then_inc(s["x_upd"], 1)
                restart()

            dve.memset(ones[:, :], 1.0).then_inc(s["ones_ready"], 1)
            step(dve.memset(ssk[:, :], 1.0))
            step(dve.memset(rv[:, :, :], 1.0))
            dve.wait_ge(s["x_in"], 16)
            norm_stats(0, nt1[:, 0:NT])
            rsqrt(rstd[:, :], nt1[:, 0:NT], NT)
            norm_tokens(0, rstd)
            dve.wait_ge(s["ctx_hi"], 1)
            dve.tensor_tensor(ctxT[:, 1], ctx32[:, :, :], ctxT[:, 0], ALU.subtract).then_inc(s["ctx_lo"], 1)
            split_lo(0)
            dve.wait_ge(s["const_in"], 16 * CONSTS)
            step(dve.tensor_scalar(cosT[:, :], cosT[:, :], qw[:, 0:1], None, ALU.mult))
            step(dve.tensor_scalar(sinT[:, :], sinT[:, :], qw[:, 1:2], None, ALU.mult))
            step(dve.tensor_tensor(cosR[:, :, :], cosR[:, :, :], rep(kw[:, 0, :], NT), ALU.mult))
            step(dve.tensor_tensor(sinR[:, :, :], sinR[:, :, :], rep(kw[:, 1, :], NT), ALU.mult))
            tokens(0)
            key_norms(0)
            scale_keys(0)
            values(0)
            split_lo(1)
            split_lo(2)
            dve.wait_ge(s["gate_tanh"], 1)
            step(dve.tensor_scalar(gscale[:, 0:1], tanhg[:, 0:1], 1.0 / (WS * WS), None, ALU.mult))
            step(dve.tensor_scalar(gscale[:, 2:4], tanhg[:, 2:4], 1.0 / (WS * HS), None, ALU.mult))
            dve.wait_ge(s["gw_hi"], 1)
            dve.scalar_tensor_tensor(out=gw0p[:, 1], in0=gw0[:, :, :], scalar=WS, in1=gw0p[:, 0],
                                     op0=ALU.mult, op1=ALU.subtract).then_inc(s["gw_lo"], 1)
            dve.wait_ge(s["x_rest_in"], 16)
            restart()
            with dve.Fori(0, B - 1) as b:
                batch(b, True)
            batch(B - 1, False)

            dve.wait_ge(s["x_upd"], B * NT)
            dve.sem_inc(s["f_h"], 2)
            ffn_split_lo(1)

            def tokens_lo(c, first, banks):
                for k in range(KC):
                    dve.wait_ge(s["fx_hi"], first + c * KC + k + 1)
                    dve.tensor_tensor(gxT[:, 1, k], banks[k][:, :], gxT[:, 0, k], ALU.subtract)\
                       .then_inc(s["fx_lo"], 1)

            def whole(out_ap, in_ap, inverse_scale):
                step(dve.tensor_scalar(out_ap, in_ap, inverse_scale, ROUND, ALU.mult, ALU.add))
                step(dve.tensor_scalar(out_ap, out_ap, ROUND, 127.0, ALU.subtract, ALU.min))

            def quantise_weights():
                dve.wait_ge(s["c1_in"], 16 * CONSTS1)
                dve.wait_ge(s["l1_in"], 16)
                step(dve.tensor_copy(gscale[:, 1:2], tanhg[:, 1:2]))
                step(dve.memset(onesM[:, :], 1.0))
                wqp = flat[:, L1_SPLIT:L1_ALL].rearrange("p (j n) -> p j n", j=4)
                step(dve.tensor_reduce(wabs[:, :], wqp, AX.X, ALU.max, apply_absolute_value=True))
                step(dve.tensor_scalar(wsc[:, :], wabs[:, :], 1.0 / 127.0, 1e-8, ALU.mult, ALU.max))
                step(dve.reciprocal(winv[:, :], wsc[:, :]))
                for j in range(4):
                    whole(wqp[:, j], wqp[:, j], winv[:, j:j + 1])
                    last = dve.tensor_scalar(diag[:, j], ident[:, :], wsc[:, j:j + 1], None, ALU.mult)
                last.then_inc(s["a_wint"], 1)

            def weight_integers():
                for j in range(2):
                    dve.wait_ge(s["a_wT"], j + 1)
                    dve.tensor_scalar(wint[:, j], TOKENS_0[j][:, :].rearrange("p (k n) -> p k n", k=KC), -127.0, None,
                                      ALU.max).then_inc(s["a_wq"], 1)

            def weight_scales():
                dve.wait_ge(s["a_srow"], 1)
                dve.tensor_copy(srow[:, :, :], bQ[:, :].rearrange("p (j n) -> p j n", j=2)).then_inc(s["a_srow_read"], 1)
                dve.wait_ge(s["a_srow_read"], 1)

            def mixture():
                step(dve.tensor_tensor(amp[:, :, :], amp[:, :, :], amp[:, :, :], ALU.mult))
                step(dve.tensor_reduce(mixp[:, :], amp[:, :, :], AX.X, ALU.add))
                step(dve.tensor_reduce(mixs[:, 0:1], mixp[:, :], AX.X, ALU.add))
                step(dve.tensor_scalar(mixs[:, 0:1], mixs[:, 0:1], EPS1, None, ALU.add))
                step(dve.reciprocal(mixs[:, 1:2], mixs[:, 0:1]))
                step(dve.tensor_scalar(mixp[:, :], mixp[:, :], mixs[:, 1:2], escale[:, 0:1], ALU.mult, ALU.mult))

            def token_stats(b):
                for t in range(NT):
                    last = dve.bn_stats(gstats[:, t, :], x[:, b * NT + t, :])
                step(last)
                for t in range(NT):
                    last = dve.bn_aggr(gmv[:, t, :], gstats[:, t, :])
                step(last)
                step(dve.tensor_scalar(gvar[:, 0:NT], gmv[:, 0:NT, 1], LN_EPS, None, ALU.add))
                group_done["n"] = 0

            def token_norms():
                group_newton(10)
                dve.wait_ge(s["dve_step"], group_done["count"])

            def token_scales(b):
                for t in range(NT):
                    last = dve.tensor_scalar(gxn[:, t, :], x[:, b * NT + t, :], gmv[:, t, 0:1], grstd[:, t:t + 1],
                                             ALU.subtract, ALU.mult)
                step(last)
                step(dve.tensor_reduce(xabs[:, :], gxn[:, 0:NT, :], AX.X, ALU.max, apply_absolute_value=True))
                step(dve.tensor_scalar(xs[:, :], xabs[:, :], 1.0 / 127.0, 1e-8, ALU.mult, ALU.max))
                step(dve.reciprocal(xsi[:, :], xs[:, :]))

            def token_integers():
                for t in range(NT):
                    last = dve.tensor_scalar(xi[:, t], gxn[:, t, :], xsi[:, t:t + 1], ROUND, ALU.mult, ALU.add)
                step(last)
                dve.tensor_scalar(xi[:, :, :], xi[:, :, :], ROUND, 127.0, ALU.subtract, ALU.min).then_inc(s["a_x"], 1)

            def group0(c, following):
                dve.wait_ge(s["f_logit"], c + 1)
                step(dve.tensor_scalar(lg[:, :, :], bM[:, 0:TG * E0].rearrange("p (t e) -> p t e", t=TG), 1.0 / WS, None,
                                       ALU.mult))
                step(dve.tensor_tensor(ld[:, :], lg[:, :, 0], lg[:, :, 1], ALU.subtract))
                step(dve.tensor_scalar(lt[:, :], ld[:, :], -1.0, None, ALU.mult))
                dve.tensor_tensor(la[:, :], ld[:, :], lt[:, :], ALU.max).then_inc(s["f_absd"], 1)
                dve.wait_ge(s["f_tanh"], c + 1)
                step(dve.tensor_scalar(topw[:, :], lt[:, :], 0.5, 0.5, ALU.mult, ALU.add))
                step(dve.scalar_tensor_tensor(out=cf[:, 0, :], in0=ld[:, :], scalar=0.0, in1=topw[:, :],
                                              op0=ALU.is_ge, op1=ALU.mult))
                step(dve.tensor_tensor(cf[:, 1, :], topw[:, :], cf[:, 0, :], ALU.subtract))
                step(dve.tensor_scalar(cfg[:, :, :], cf[:, :, :], gscale[:, 2:3], None, ALU.mult))
                U = E0 * FC
                for u in range(U + 3):
                    if u < U:
                        dve.wait_ge(s["f_silu"], c * U + u + 1)
                        dve.wait_ge(s["fu_mm"], c * U + u + 1)
                        if u >= 2:
                            dve.wait_ge(s["f_hlo"], c * U + u - 1)
                        dve.scalar_tensor_tensor(out=hh32[:, u % 2, :], in0=[bPa, bPb][u % 2][:, :], scalar=HS / WS,
                                                 in1=sg[:, u % 2, :], op0=ALU.mult, op1=ALU.mult).then_inc(s["f_h"], 1)
                    if 1 <= u <= U:
                        dve.wait_ge(s["f_hhi"], c * U + u)
                        dve.tensor_tensor(hT[:, (u - 1) % 4, 1, :], hh32[:, (u - 1) % 2, :], hT[:, (u - 1) % 4, 0, :],
                                          ALU.subtract).then_inc(s["f_hlo"], 1)
                    if following:
                        if u == 2:
                            group_stats(c + 1)
                        if u == 3:
                            group_norms()
                        if u == 4:
                            group_scales(c + 1)
                        if u == U + 1:
                            tokens_lo(c + 1, 0, TOKENS_0)
                    else:
                        if u == 2:
                            quantise_weights()
                        if u == 4:
                            mixture()
                        if u == FC + 2:
                            weight_integers()
                        if u == FC + 4:
                            weight_scales()
                        if u == FC + 5:
                            token_stats(0)
                        if u == FC + 6:
                            token_norms()
                        if u == FC + 7:
                            token_scales(0)
                            token_integers()
                    if u - 2 in (FC - 1, U - 1):
                        e = (u - 2) // FC
                        dve.wait_ge(s["f_down"], c * U + e * FC + FC + 4)
                        for t in range(TG):
                            if e:
                                dve.wait_ge(s["f_upd"], c * TG * E0 + t + 2)
                            y = [bV, bR][t // 2][:, (t % 2) * DM:(t % 2 + 1) * DM]
                            dve.scalar_tensor_tensor(out=x[:, c * TG + t, :], in0=y, scalar=cfg[:, e, t:t + 1],
                                                     in1=x[:, c * TG + t, :], op0=ALU.mult, op1=ALU.add)\
                               .then_inc(s["f_upd"], 1)
                restart()

            dve.sem_inc(s["f_upd"], 1)
            tokens_lo(0, 0, TOKENS_0)
            ffn_split_lo(2)
            restart()
            with dve.Fori(0, NG - 1) as c:
                group0(c, True)
            group0(NG - 1, False)

            dve.wait_ge(s["lw_hi"], 1)
            dve.scalar_tensor_tensor(out=flatp[:, L1_SPLIT:L1_SPLIT + L1_KV], in0=flat[:, 0:L1_KV], scalar=WS,
                                     in1=flatp[:, 0:L1_KV], op0=ALU.mult, op1=ALU.subtract).then_inc(s["lw_lo"], 1)
            for k in range(KC):
                dve.wait_ge(s["a_k"], k + 1)
                dve.tensor_scalar(k1[:, k], [bPb, bPa][k][:, :], 1.0 / WS, bk[:, k:k + 1], ALU.mult, ALU.add)\
                   .then_inc(s["a_k1"], 1)
            dve.wait_ge(s["a_khi"], 1)
            dve.tensor_tensor(k1p[:, 1], k1[:, :, :], k1p[:, 0], ALU.subtract).then_inc(s["a_klo"], 1)
            dve.wait_ge(s["f_upd"], NG * TG * E0 + 1)

            def token_transposes(b):
                dve.wait_ge(s["a_xT"], b + 1)
                dve.tensor_scalar(xqT[:, :, :], bM[:, :].rearrange("p (k n) -> p k n", k=KC), -127.0, None, ALU.max)\
                   .then_inc(s["a_xq"], 1)

            def values1(b):
                dve.wait_ge(s["a_v"], b + 1)
                step(dve.scalar_tensor_tensor(out=v1[:, :], in0=bV[:, 0:DM], scalar=1.0 / WS, in1=rows1[:, 2, :],
                                              op0=ALU.mult, op1=ALU.add))
                vv = v1[:, :].rearrange("p (m s d) -> p m s d", m=H1 // 2, s=2)
                for half in range(2):
                    last = dve.tensor_scalar(vv[:, :, half], vv[:, :, half], keymask[:, half:half + 1], None, ALU.mult)
                last.then_inc(s["a_v1"], 1)

            def queries1(b):
                dve.wait_ge(s["a_q"], b + 1)
                for t in range(NT):
                    last = dve.scalar_tensor_tensor(out=q1[:, t], in0=bM[:, t * DM:(t + 1) * DM], scalar=xs[:, t:t + 1],
                                                    in1=srow[:, 0, :], op0=ALU.mult, op1=ALU.mult)
                step(last)
                dve.tensor_tensor(q1[:, :, :], q1[:, :, :], rep(rows1[:, 0, :], NT), ALU.add).then_inc(s["a_q1"], 1)

            def queries1_lo(b):
                dve.wait_ge(s["a_qhi"], b + 1)
                dve.tensor_tensor(q1T[:, 1], bV[:, :].rearrange("p (k n) -> p k n", k=KC), q1T[:, 0], ALU.subtract)\
                   .then_inc(s["a_qlo"], 1)

            def values1_lo(b):
                dve.wait_ge(s["a_vhi"], b + 1)
                dve.tensor_tensor(vbd[:, 1, :], v1[:, :], vbd[:, 0, :], ALU.subtract).then_inc(s["a_vlo"], 1)

            def split_rest(n):
                dve.wait_ge(s["lr_hi"], 1)
                third = (L1_SPLIT - L1_KV) // 3
                at = L1_KV + n * third
                dve.scalar_tensor_tensor(out=flatp[:, L1_SPLIT + at:L1_SPLIT + at + third], in0=flat[:, at:at + third],
                                         scalar=WS, in1=flatp[:, at:at + third], op0=ALU.mult, op1=ALU.subtract)\
                   .then_inc(s["lr_lo"], 1)

            def batch1(b, following):
                def inverse1(u):
                    dve.wait_ge(s["a_exp"], 4 * b + u + 1)
                    step(dve.reciprocal(ei1[:, u, :], es1[:, u, :]))
                    dve.tensor_scalar(ei1[:, u, :], ei1[:, u, :], PS, None, ALU.mult).then_inc(s["a_inv"], 1)

                def probs1_lo(u):
                    dve.wait_ge(s["a_pthi"], 4 * b + u + 1)
                    dve.tensor_tensor(pt1[:, u, 1], [bR, bQ][u % 2][:, :].rearrange("p (m n) -> p m n", m=4),
                                      pt1[:, u, 0], ALU.subtract).then_inc(s["a_ptlo"], 1)

                for u in range(4):
                    dve.wait_ge(s["a_s"], 4 * b + u + 1)
                    step(dve.tensor_reduce(mx1[:, u, :], UNIT_S[u][:, :].rearrange("p (h n) -> p h n", h=HC), AX.X,
                                           ALU.max))
                    dve.tensor_scalar(mx1[:, u, :], mx1[:, u, :], -float(D1) ** -0.5, None, ALU.mult)\
                       .then_inc(s["a_e"], 1)
                if following:
                    token_stats(b + 1)
                else:
                    split_rest(0)
                inverse1(0)
                if following:
                    token_norms()
                else:
                    split_rest(1)
                inverse1(1)
                if following:
                    token_scales(b + 1)
                else:
                    split_rest(2)
                inverse1(2)
                if following:
                    token_integers()
                else:
                    dve.wait_ge(s["a_upd"], TG // NT + 1)
                    group_stats(0)
                inverse1(3)
                probs1_lo(0)
                if following:
                    token_transposes(b + 1)
                probs1_lo(1)
                probs1_lo(2)
                if following:
                    values1(b + 1)
                else:
                    group_norms()
                    group_scales(0)
                probs1_lo(3)
                if following:
                    queries1(b + 1)
                for t in range(NT):
                    dve.wait_ge(s["a_o"], NT * b + t + 1)
                    last = dve.tensor_reduce(oabs[:, t:t + 1], bS[t][:, 0:DM], AX.X, ALU.max, apply_absolute_value=True)
                step(last)
                step(dve.tensor_scalar(os1[:, :], oabs[:, :], 1.0 / 127.0, PS * 1e-8, ALU.mult, ALU.max))
                step(dve.reciprocal(osi[:, :], os1[:, :]))
                for t in range(NT):
                    last = dve.tensor_scalar(oi[:, t], bS[t][:, 0:DM], osi[:, t:t + 1], ROUND, ALU.mult, ALU.add)
                step(last)
                dve.tensor_scalar(oi[:, :, :], oi[:, :, :], ROUND, 127.0, ALU.subtract, ALU.min).then_inc(s["a_oi"], 1)
                step(dve.tensor_scalar(os1[:, :], os1[:, :], 1.0 / PS, None, ALU.mult))
                if following:
                    queries1_lo(b + 1)
                dve.wait_ge(s["a_oT"], b + 1)
                dve.tensor_scalar(oqT[:, :, :], bPa[:, :].rearrange("p (k n) -> p k n", k=KC), -127.0, None, ALU.max)\
                   .then_inc(s["a_oq"], 1)
                if following:
                    values1_lo(b + 1)
                dve.wait_ge(s["a_y"], b + 1)
                for t in range(NT):
                    last = dve.scalar_tensor_tensor(out=y1[:, t], in0=bPb[:, t * DM:(t + 1) * DM], scalar=os1[:, t:t + 1],
                                                    in1=srow[:, 1, :], op0=ALU.mult, op1=ALU.mult)
                step(last)
                step(dve.tensor_tensor(y1[:, :, :], y1[:, :, :], rep(rows1[:, 1, :], NT), ALU.add))
                xb = x[:, bass.ds(b * NT, NT), :].rearrange("p t n -> p (t n)")
                dve.scalar_tensor_tensor(out=xb, in0=sg[:, 1, :], scalar=gscale[:, 1:2],
                                         in1=xb, op0=ALU.mult, op1=ALU.add).then_inc(s["a_upd"], 1)
                restart()

            dve.sem_inc(s["a_upd"], 1)
            token_transposes(0)
            values1(0)
            queries1(0)
            values1_lo(0)
            queries1_lo(0)
            dve.wait_ge(s["a_qlo"], 1)
            restart()
            with dve.Fori(0, B - 1) as b:
                batch1(b, True)
            batch1(B - 1, False)

            dve.wait_ge(s["a_upd"], B + 1)
            dve.sem_inc(s["m_h"], 2)
            dve.sem_inc(s["m_upd"], 1)

            def router_logits(c):
                lgt = bR[:, :].rearrange("p (t e) -> p t e", t=TG)
                dve.wait_ge(s["r_logit"], c + 1)
                step(dve.tensor_reduce(rmx[:, :], lgt, AX.X, ALU.max))
                dve.tensor_tensor(rex[:, :, :], lgt, spread(rmx[:, :], E1), ALU.subtract).then_inc(s["r_e"], 1)

            def router_top(c):
                dve.wait_ge(s["r_exp"], c + 1)
                step(dve.tensor_reduce(rsum[:, :], rex[:, :, :], AX.X, ALU.add))
                step(dve.reciprocal(rinv[:, :], rsum[:, :]))
                step(dve.tensor_tensor(rex[:, :, :], rex[:, :, :], spread(rinv[:, :], E1), ALU.mult))
                for t in range(TG):
                    last = dve.max(top8[:, t, :], rex[:, t, :])
                step(last)
                for t in range(TG):
                    last = dve.max_index(idx8[:, t, :], top8[:, t, :], rex[:, t, :])
                step(last)

            def router_weights(c):
                step(dve.tensor_copy(idxf[:, :, :], idx8[:, :, :]))
                step(dve.tensor_reduce(tw[:, :], top8[:, :, 0:4], AX.X, ALU.add))
                step(dve.tensor_scalar(tw[:, :], tw[:, :], EPS1, None, ALU.add))
                step(dve.reciprocal(tw[:, :], tw[:, :]))
                for k in range(4):
                    for t in range(TG):
                        if k == 0:
                            last = dve.tensor_scalar(chosen[:, t, :], iota[:, :], idxf[:, t, 0:1], None, ALU.is_equal)
                        else:
                            last = dve.scalar_tensor_tensor(out=chosen[:, t, :], in0=iota[:, :],
                                                            scalar=idxf[:, t, k:k + 1], in1=chosen[:, t, :],
                                                            op0=ALU.is_equal, op1=ALU.add)
                    step(last)
                for t in range(TG):
                    last = dve.scalar_tensor_tensor(out=chosen[:, t, :], in0=chosen[:, t, :], scalar=tw[:, t:t + 1],
                                                    in1=rex[:, t, :], op0=ALU.mult, op1=ALU.mult)
                last.then_inc(s["r_w"], 1)

            def router_mixture(c):
                dve.wait_ge(s["r_wT"], c + 1)
                dve.tensor_copy(WT[:, :], bR[:, :]).then_inc(s["r_wTc"], 1)
                dve.wait_ge(s["r_c"], c + 1)
                dve.tensor_copy(cc[:, :, :], bR[:, 0:TG * KB].rearrange("p (t k) -> p t k", t=TG)).then_inc(s["r_cc"], 1)

            def hidden1(c, u):
                dve.wait_ge(s["m_silu"], c * U1 + u + 1)
                dve.wait_ge(s["m_u"], c * U1 + u + 1)
                dve.scalar_tensor_tensor(out=hh32[:, u % 2, :], in0=[bPa, bPb][u % 2][:, :], scalar=HS / WS,
                                         in1=sg[:, u % 2, :], op0=ALU.mult, op1=ALU.mult).then_inc(s["m_h"], 1)

            places = [mixed, e1[:, 0].rearrange("p h n -> p (h n)").rearrange("p (t i) -> p t i", t=TG)]
            written = {}

            def mix1(c, u, between):
                dve.wait_ge(s["m_h"], c * U1 + u + 3)
                if u == 2:
                    dve.wait_ge(s["r_cc"], c + 1)
                t, half = (u - 2) // 2, (u - 2) % 2
                for k in range(4):
                    base = hh32[:, u % 2, k * I1:(k + 1) * I1]
                    w = cc[:, t, half * 4 + k:half * 4 + k + 1]
                    place = places[k % 2][:, t, :]
                    if half == 0 and k < 2:
                        ins = dve.tensor_scalar(place, base, w, None, ALU.mult)
                    else:
                        dve.wait_ge(s["dve_step"], written[k % 2])
                        ins = dve.scalar_tensor_tensor(out=place, in0=base, scalar=w, in1=place, op0=ALU.mult,
                                                       op1=ALU.add)
                    written[k % 2] = mark(ins)
                    if between:
                        group_newton(group_done["n"] + 1)

            def mixed_sum(u):
                t = (u - 2) // 2
                dve.wait_ge(s["dve_step"], max(written.values()))
                ins = dve.tensor_tensor(mixed[:, t, :], places[0][:, t, :], places[1][:, t, :], ALU.add)
                if u == U1 - 1:
                    ins.then_inc(s["m_mixed"], 1)

            def mixed_lo(c):
                dve.wait_ge(s["m_mhi"], c + 1)
                dve.tensor_tensor(mT[:, 1], bQ[:, :], mT[:, 0], ALU.subtract).then_inc(s["m_mlo"], 1)

            def update1(c):
                for t in range(TG):
                    dve.wait_ge(s["m_y"], c * 2 + t // 2 + 1)
                    dve.scalar_tensor_tensor(out=x[:, bass.ds(c * TG + t, 1), :].rearrange("p o n -> p (o n)"),
                                             in0=[bV, bM][t // 2][:, (t % 2) * DM:(t % 2 + 1) * DM],
                                             scalar=gscale[:, 3:4],
                                             in1=x[:, bass.ds(c * TG + t, 1), :].rearrange("p o n -> p (o n)"),
                                             op0=ALU.mult, op1=ALU.add).then_inc(s["m_upd"], 1)

            def front1(c, first):
                tokens_lo(c, NG * KC, TOKENS_1)
                if not first:
                    mixed_sum(U1 - 1)
                router_logits(c)
                if not first:
                    mixed_lo(c - 1)
                router_top(c)
                for u in range(2):
                    hidden1(c, u)
                    dve.wait_ge(s["m_hi"], c * 2 + u + 1)
                    dve.tensor_tensor(hT[:, u, 1, :], hh32[:, u % 2, :], hT[:, u, 0, :], ALU.subtract)\
                       .then_inc(s["m_lo"], 1)
                if not first:
                    update1(c - 1)
                router_weights(c)
                router_mixture(c)

            def group1(c, following):
                for u in range(2, U1):
                    hidden1(c, u)
                    if u > 2 and u % 2 == 0:
                        mixed_sum(u - 1)
                    mix1(c, u, following and 4 <= u <= 6)
                    if following:
                        if u == 3:
                            group_stats(c + 1)
                            group_done["n"] = 0
                        if u == 6:
                            dve.wait_ge(s["dve_step"], group_done["count"])
                            group_scales(c + 1)
                if following:
                    front1(c + 1, False)
                else:
                    mixed_sum(U1 - 1)
                restart()

            front1(0, True)
            restart()
            with dve.Fori(0, NG - 1) as c:
                group1(c, True)
            group1(NG - 1, False)
            mixed_lo(NG - 1)
            update1(NG - 1)

        @block.gpsimd
        def _(pool):
            pool.sem_inc(s["q_lo"], 2)
            pool.sem_inc(s["o_lo"], 2)

            def hold():
                pool.sem_inc(s["pool_held"], 1)

            def keys(b):
                for n in range(3):
                    r = ROWS[n]
                    pool.wait_ge(s["kn_ready"], b * 3 + n + 1)
                    if n == 0:
                        pool.tensor_tensor(kr[0:r, n], kn[0:r, n], rep(kw[0:r, 0, :], G), ALU.mult)\
                            .then_inc(s["kr_ready"], 1)
                    else:
                        pool.tensor_tensor(kr[:, n], kn[:, n], rep(cosR[:, n - 1, :], G), ALU.mult)\
                            .then_inc(s["kc_mul"], 1)
                        pool.wait_ge(s["ks_mul"], b * 2 + n)
                        pool.wait_ge(s["kc_mul"], b * 2 + n)
                        pool.tensor_tensor(kr[:, n], kr[:, n], ks[:, n - 1], ALU.add).then_inc(s["kr_ready"], 1)

            def batch(b, following):
                def rope(i):
                    j = i % 2
                    pool.wait_ge(s["q_rope"], b * HP + i + 1)
                    pool.tensor_tensor(qa[:, j], qa[:, j], qs[:, j], ALU.add).then_inc(s["pool_step"], 1)
                    pool.wait_ge(s["pool_step"], b * HP + i + 1)
                    if i >= 2:
                        pool.wait_ge(s["s_mm"], b * H + 2 * (i - 2) + 2)
                    hold()
                    pool.tensor_scalar(qT[:, j, 0], qa[:, j], 1.0, 1.0, ALU.mult, ALU.mult).then_inc(s["q_hi"], 1)
                    pool.wait_ge(s["q_hi"], b * HP + i + 1)
                    pool.tensor_tensor(qT[:, j, 1], qa[:, j], qT[:, j, 0], ALU.subtract).then_inc(s["q_lo"], 1)

                def normalise(i):
                    pool.wait_ge(s["inv_ready"], b * HP + i + 1)
                    hold()
                    for hh in range(2):
                        for t in range(NT):
                            a = p[:, i % 2, hh, AT[t]:AT[t] + SPAN[t]]
                            last = pool.tensor_scalar(a, a, einv[:, i % 2, 2 * hh + t:2 * hh + t + 1], PS,
                                                      ALU.mult, ALU.mult)
                    last.then_inc(s["p_norm"], 1)

                def out_lo(g):
                    for n, t in enumerate(TILES):
                        pool.wait_ge(s["o_hi"], b * 2 * G + 2 * g + n + 1)
                        heads, cols = slice(4 * g, 4 * g + 4), slice(t * P, (t + 1) * P)
                        pool.tensor_tensor(oT[:, 1, heads, cols], o32[:, t], oT[:, 0, heads, cols], ALU.subtract)\
                            .then_inc(s["o_lo"], 1)

                for i in range(HP + 2):
                    if i >= 2:
                        normalise(i - 2)
                    if i < HP:
                        rope(i)
                    if i >= 6 and i % 2 == 0:
                        out_lo((i - 6) // 2)
                out_lo(G - 2)
                out_lo(G - 1)
                if following:
                    keys(b + 1)

            keys(0)
            with pool.Fori(0, B - 1) as b:
                batch(b, True)
            batch(B - 1, False)

            pool.wait_ge(s["a_klo"], 1)

            def keys1(b):
                for j in range(2):
                    for rpt in range(2):
                        last = pool.tensor_copy(ctxd[:, j, :, rpt, :], ctxT[:, j, :, bass.ds(b * T, T)])
                last.then_inc(s["a_ctx"], 1)
                for j in range(2):
                    for k in range(KC):
                        last = pool.tensor_tensor(kbd[:, j, k], rep(k1p[:, j, k, bass.ds(b * T, T)], HC),
                                                  spread(headmask[:, :], T), ALU.mult)
                last.then_inc(s["a_kbd"], 1)

            def batch1(b, following):
                for u in range(4):
                    pool.wait_ge(s["a_inv"], 4 * b + u + 1)
                    pool.tensor_tensor(e1[:, u], e1[:, u], spread(ei1[:, u, :], T), ALU.mult).then_inc(s["a_p"], 1)
                if following:
                    keys1(b + 1)

            keys1(0)
            with pool.Fori(0, B - 1) as b:
                batch1(b, True)
            batch1(B - 1, False)

        @block.tensor
        def _(pe):
            pe.sem_inc(s["q_mm"], 1)
            pe.sem_inc(s["ssq_mm"], 1)
            pe.sem_inc(s["pt_mm"], 4)
            pe.sem_inc(s["pv_mm"], 4)
            pe.wait_ge(s["const_in"], 16 * CONSTS)
            pe.wait_ge(s["ones_ready"], 1)
            def tokens(b, first):
                pe.wait_ge(s["xn_ready"], b + 1)
                if not first:
                    pe.wait_ge(s["q_sq"], b * HP - 1)
                for k in range(KC):
                    for t in range(NT):
                        last = pe.transpose(bQ[:, k * L + t * P:k * L + (t + 1) * P],
                                            xn[:, t, k * P:(k + 1) * P], ident[:, :])
                last.then_inc(s["xnT_mm"], 1)

            def key_values(b, which, first):
                for n in range(3):
                    if n == 0 and which == 0:
                        pe.wait_ge(s["ctx_copy"], b + 1)
                    if n == 0 and not first:
                        if which == 0:
                            pe.wait_ge(s["exp_done"], b * H)
                        else:
                            pe.wait_ge(s["q_sq"], b * HP)
                            pe.wait_ge(s["pt_lo"], b * 2 * HP)
                    if n == 1 and which == 0:
                        pe.wait_ge(s["xT_lo"], b + 1)
                    bank = [K_BANK, V_BANK][which][n]
                    w = 2 * (n > 0) + which
                    for k in range(KC):
                        if n == 0:
                            src = [ctxb[:, j, k, 0:1 + which, :].rearrange("p r n -> p (r n)") for j in range(2)]
                        else:
                            src = [xT[:, j, k, (n - 1) * P:n * P] for j in range(2)]
                        last = product(pe, bank[0:[ROWS, V_ROWS][which][n], :], src, [wkv[:, j, w, k, :] for j in range(2)],
                                       k == 0, k == KC - 1)
                    last.then_inc(s["kv_mm"], 1)

            def keys(b):
                for g in range(G):
                    if g == 0:
                        pe.wait_ge(s["kr_ready"], b * 3 + 3)
                    if g == 2:
                        pe.wait_ge(s["v_lo"], b * 3 + 3)
                    for n in (1, 0, 2):
                        last = pe.transpose(KT_BANK[g][:, COL[n]:COL[n] + ROWS[n]], kr[0:ROWS[n], n, g, :],
                                            ident[0:ROWS[n], 0:ROWS[n]])
                    last.then_inc(s["kT_mm"], 1)

            def batch(b, first, following):
                def project(i):
                    if i >= 2:
                        pe.wait_ge(s["q_sq"], b * HP + i - 1)
                    elif i == 1:
                        pe.wait_ge(s["v_lo"], b * 3 + 1)
                    else:
                        pe.wait_ge(s["kn_ready"], b * 3 + 3)
                    for hh in range(2):
                        h = 2 * i + hh
                        for k in range(KC):
                            last = product(pe, Q_BANK[i % 2][:, hh * L:(hh + 1) * L], [wq[:, j, k, h * D:(h + 1) * D] for j in range(2)],
                                           [xT[:, j, k, :] for j in range(2)], k == 0, k == KC - 1)
                    last.then_inc(s["q_mm"], 1)

                def scores(i):
                    pe.wait_ge(s["q_lo"], b * HP + i + 3)
                    if i == 0:
                        pe.wait_ge(s["kT_lo"], b * G + G)
                    g = i // 2
                    for hh in range(2):
                        if i:
                            pe.wait_ge(s["exp_done"], b * H + 2 * i - 1 + hh)
                        for t in range(NT):
                            o = bS[hh][:, AT[t]:AT[t] + SPAN[t]]
                            query = [qT[:, i % 2, j, hh, t * P:(t + 1) * P] for j in range(2)]
                            if t == 0:
                                product(pe, o[:, P:P + T], query, [kT[:, j, g, 0:T] for j in range(2)], True, True)
                                product(pe, o[:, 0:P], query, [kT[:, j, g, T:T + P] for j in range(2)], True, False)
                                diagonal = o[:, 0:P]
                            else:
                                product(pe, o, query, [kT[:, j, g, 0:SPAN[t]] for j in range(2)], True, False)
                                diagonal = o[:, L - P + T:L + T]
                            last = pe.matmul(diagonal, identb[:, :], maskb[:, :], start=False, stop=True,
                                             skip_group_check=True)
                        last.then_inc(s["s_mm"], 1)

                def sums(i):
                    pe.wait_ge(s["q_sq"], b * HP + i + 1)
                    if i == 0:
                        if not first:
                            pe.wait_ge(s["x_upd"], b * NT)
                    else:
                        pe.wait_ge(s["ssq_read"], b * HP + i)
                    if i >= 5:
                        pe.wait_ge(s["o_hi"], b * 2 * G + 2 * ((i - 5) // 2) + 1)
                    for hh in range(2):
                        for t in range(NT):
                            c = 2 * hh + t
                            last = pe.matmul(bM[:, c:c + 1], sq[:, hh * L + t * P:hh * L + (t + 1) * P], ones[:, :],
                                             start=True, stop=True, skip_group_check=True)
                    last.then_inc(s["ssq_mm"], 1)

                def transpose_probs(i):
                    pe.wait_ge(s["p_norm"], b * HP + i + 1)
                    pv = p[:, i % 2]
                    if i == 0:
                        pe.wait_ge(s["kT_lo"], b * G + G)
                    else:
                        pe.wait_ge(s["pt_lo"], b * 2 * HP + 2 * i)
                    for j, bank in enumerate((bPa, bPb)):
                        for k in range(2):
                            for hh in range(2):
                                c, at = (k * 2 + hh) * P, (2 * j + k) * P
                                last = pe.transpose(bank[:, c:c + P], pv[:, hh, at:at + P], ident[:, :])
                        last.then_inc(s["pt_mm"], 1)

                def attend(g):
                    pe.wait_ge(s["pt_lo"], b * 2 * HP + 4 * g + 4)
                    for t in TILES:
                        if t == 0:
                            if g:
                                pe.wait_ge(s["o_hi"], b * 2 * G + 2 * g)
                        else:
                            pe.wait_ge(s["ssq_read"], b * HP + min(2 * g + 5, HP))
                        o = [bV, bM][t][:, :]
                        if t == 0:
                            blocks = [(slice(0, P), 1, pta, 0), (slice(0, T), 0, pta, 1)]
                        else:
                            blocks = [(slice(T, P), 0, pta, 1), (slice(0, P), 1, ptb, 0), (slice(0, P), 2, ptb, 1)]
                        for m, (r, n, pt, k) in enumerate(blocks):
                            last = product(pe, o, [v[r, j, n, g * D:(g + 1) * D] for j in range(2)],
                                           [pt[r, g % 2, j, k].rearrange("p h n -> p (h n)") for j in range(2)],
                                           m == 0, m == len(blocks) - 1)
                        last.then_inc(s["pv_mm"], 1)

                for i in range(HP + 4):
                    if 0 <= i - 2 < HP:
                        scores(i - 2)
                    if 2 <= i <= HP:
                        sums(i - 1)
                    if i < HP:
                        project(i)
                    if i == 0:
                        keys(b)
                    if i == 1:
                        sums(0)
                    if 0 <= i - 3 < HP:
                        transpose_probs(i - 3)
                    if i == HP and following:
                        tokens(b + 1, False)
                    if i == HP + 2 and following:
                        key_values(b + 1, 0, False)
                    if i >= 5 and i % 2 == 1:
                        attend((i - 5) // 2)
                if following:
                    key_values(b + 1, 1, False)
                pe.wait_ge(s["stage_free"], 3)
                pe.wait_ge(s["o_lo"], b * 2 * G + 2 * G + 2)
                for t in range(NT):
                    for h in range(H):
                        last = product(pe, [bV, bM][t][:, 0:DM], [oT[:, j, h, t * P:(t + 1) * P] for j in range(2)],
                                       [wo[:, j, h, :] for j in range(2)], h == 0, h == H - 1)
                    last.then_inc(s["wo_mm"], 1)

            tokens(0, True)
            pe.wait_ge(s["ctx_lo"], 1)
            pe.wait_ge(s["stage_free"], 1)
            key_values(0, 0, True)
            key_values(0, 1, True)
            pe.wait_ge(s["stage_free"], 2)
            batch(0, True, True)
            with pe.Fori(1, B - 1) as b:
                batch(b, False, True)
            batch(B - 1, False, False)

            pe.sem_inc(s["f_down"], 4)
            pe.wait_ge(s["gw_lo"], 1)
            pe.wait_ge(s["x_upd"], B * NT)

            def transpose_tokens(c, first, banks):
                pe.wait_ge(s["fx_ready"], first + c + 1)
                for k in range(KC):
                    for t in range(TG):
                        last = pe.transpose(banks[k][:, t * P:(t + 1) * P], gxn[:, t, k * P:(k + 1) * P], ident[:, :])
                    last.then_inc(s["fx_mm"], 1)

            def down0(c, u):
                U = E0 * FC
                e, f = u // FC, u % FC
                pe.wait_ge(s["f_hlo"], c * U + u + 1)
                if u == 0:
                    pe.wait_ge(s["fw_lo"], 3)
                if f == 0:
                    pe.wait_ge(s["f_upd"], c * TG * E0 + e * TG + 1)
                for t in range(TG):
                    y = [bV, bR][t // 2][:, (t % 2) * DM:(t % 2 + 1) * DM]
                    last = product(pe, y, [hT[:, u % 4, j, t * P:(t + 1) * P] for j in range(2)],
                                   [wd0[:, j, e, f, :] for j in range(2)], f == 0 and t % 2 == 0, f == FC - 1)
                last.then_inc(s["f_down"], 1)

            def transpose_weights():
                pe.wait_ge(s["a_wint"], 1)
                wqp = flat[:, L1_SPLIT:L1_ALL].rearrange("p (j o n) -> p j o n", j=2, o=KC)
                for j in range(2):
                    for k in range(KC):
                        for o in range(KC):
                            last = pe.transpose(TOKENS_0[j][:, k * DM + o * P:k * DM + (o + 1) * P],
                                                wqp[:, j, o, k * P:(k + 1) * P], ident[:, :])
                    last.then_inc(s["a_wT"], 1)

            def spread_scales():
                pe.wait_ge(s["a_wq"], 2)
                for j in range(4):
                    last = pe.matmul(bQ[:, j * P:(j + 1) * P], onesM[:, :], diag[:, j, :], start=True, stop=True,
                                     skip_group_check=True)
                last.then_inc(s["a_srow"], 1)

            def group0(c, following):
                pe.wait_ge(s["fx_lo"], c * KC + KC)
                for t in range(TG):
                    for k in range(KC):
                        last = product(pe, bM[:, t * E0:(t + 1) * E0], [gxT[:, j, k, t * P:(t + 1) * P] for j in range(2)],
                                       [gw0p[:, j, k, :] for j in range(2)], k == 0, k == KC - 1)
                last.then_inc(s["f_logit"], 1)
                U = E0 * FC
                for u in range(U + 2):
                    if u < U:
                        e, f = u // FC, u % FC
                        pe.wait_ge(s["f_h"], c * U + u + 1)
                        for w, bank, done in ((wg0, bS[u % 2], "fg_mm"), (wu0, [bPa, bPb][u % 2], "fu_mm")):
                            if u == 0:
                                pe.wait_ge(s["fw_lo"], 1 if done == "fg_mm" else 2)
                            for k in range(KC):
                                last = product(pe, bank[:, :], [w[:, j, e, k, f * P:(f + 1) * P] for j in range(2)],
                                               [gxT[:, j, k, :] for j in range(2)], k == 0, k == KC - 1)
                            last.then_inc(s[done], 1)
                    if following and u == FC:
                        transpose_tokens(c + 1, 0, TOKENS_0)
                    if not following:
                        if u == FC:
                            transpose_weights()
                        if u == FC + 3:
                            spread_scales()
                    if u >= 2:
                        down0(c, u - 2)

            transpose_tokens(0, 0, TOKENS_0)
            with pe.Fori(0, NG - 1) as c:
                group0(c, True)
            group0(NG - 1, False)

            pe.wait_ge(s["lw_lo"], 1)
            wkv1 = w1("kv", KC)
            for m in range(KC):
                for k in range(KC):
                    last = product(pe, [bPb, bPa][m][:, :], [wkv1[j][:, k, m * P:(m + 1) * P] for j in range(2)],
                                   [ctxT[:, j, k, :] for j in range(2)], k == 0, k == KC - 1)
                last.then_inc(s["a_k"], 1)

            def token_transposes(b):
                pe.wait_ge(s["a_x"], b + 1)
                for k in range(KC):
                    for t in range(NT):
                        last = pe.transpose(bM[:, k * L + t * P:k * L + (t + 1) * P], xi[:, t, k * P:(k + 1) * P],
                                            ident[:, :])
                last.then_inc(s["a_xT"], 1)

            def queries1(b):
                pe.wait_ge(s["a_xq"], b + 1)
                for t in range(NT):
                    for k in range(KC):
                        last = pe.matmul(bM[:, t * DM:(t + 1) * DM], xqT[:, k, t * P:(t + 1) * P], wint[:, 0, k, :],
                                         start=(k == 0), stop=(k == KC - 1), skip_group_check=True)
                last.then_inc(s["a_q"], 1)

            def values1(b):
                pe.wait_ge(s["a_ctx"], b + 1)
                for k in range(KC):
                    last = product(pe, bV[:, 0:DM], [ctxd[:, j, k].rearrange("p r n -> p (r n)") for j in range(2)],
                                   [wkv1[j][:, k, DM:2 * DM] for j in range(2)], k == 0, k == KC - 1)
                last.then_inc(s["a_v"], 1)

            def query_transposes(b):
                pe.wait_ge(s["a_v1"], b + 1)
                pe.wait_ge(s["a_q1"], b + 1)
                for k in range(KC):
                    for t in range(NT):
                        last = pe.transpose(bV[:, k * L + t * P:k * L + (t + 1) * P], q1[:, t, k * P:(k + 1) * P],
                                            ident[:, :])
                last.then_inc(s["a_q1T"], 1)

            def batch1(b, following):
                pe.wait_ge(s["a_qlo"], b + 1)
                pe.wait_ge(s["a_kbd"], b + 1)
                for u in range(4):
                    t, k = u // 2, u % 2
                    if u == 3:
                        pe.wait_ge(s["a_upd"], b + 1)
                    product(pe, UNIT_S[u][:, :], [q1T[:, j, k, t * P:(t + 1) * P] for j in range(2)],
                            [kbd[:, j, k].rearrange("p h n -> p (h n)") for j in range(2)], True, True)\
                        .then_inc(s["a_s"], 1)

                def transpose_probs1(u):
                    pe.wait_ge(s["a_p"], 4 * b + u + 1)
                    if u >= 2:
                        pe.wait_ge(s["a_ptlo"], 4 * b + u - 1)
                    flat_e = e1[:, u].rearrange("p h n -> p (h n)")
                    for m in range(4):
                        last = pe.transpose([bR, bQ][u % 2][:, m * P:(m + 1) * P], flat_e[:, m * P:(m + 1) * P],
                                            ident[:, :])
                    last.then_inc(s["a_pt"], 1)

                def attend1(u):
                    t, k = u // 2, u % 2
                    pe.wait_ge(s["a_ptlo"], 4 * b + u + 1)
                    if u == 0:
                        pe.wait_ge(s["a_vlo"], b + 1)
                    for m in range(4):
                        c = k * P + m * 2 * D1
                        last = product(pe, bS[t][:, c:c + 2 * D1], [pt1[:, u, j, m, :] for j in range(2)],
                                       [vbd[:, j, c:c + 2 * D1] for j in range(2)], True, True)
                    if k == KC - 1:
                        last.then_inc(s["a_o"], 1)

                transpose_probs1(0)
                transpose_probs1(1)
                if following:
                    token_transposes(b + 1)
                attend1(0)
                transpose_probs1(2)
                if following:
                    queries1(b + 1)
                    values1(b + 1)
                attend1(1)
                transpose_probs1(3)
                attend1(2)
                attend1(3)
                if following:
                    query_transposes(b + 1)
                pe.wait_ge(s["a_oi"], b + 1)
                for k in range(KC):
                    for t in range(NT):
                        last = pe.transpose(bPa[:, k * L + t * P:k * L + (t + 1) * P], oi[:, t, k * P:(k + 1) * P],
                                            ident[:, :])
                last.then_inc(s["a_oT"], 1)
                pe.wait_ge(s["a_oq"], b + 1)
                for t in range(NT):
                    for k in range(KC):
                        last = pe.matmul(bPb[:, t * DM:(t + 1) * DM], oqT[:, k, t * P:(t + 1) * P], wint[:, 1, k, :],
                                         start=(k == 0), stop=(k == KC - 1), skip_group_check=True)
                last.then_inc(s["a_y"], 1)

            token_transposes(0)
            pe.wait_ge(s["a_klo"], 1)
            pe.wait_ge(s["f_upd"], NG * TG * E0 + 1)
            values1(0)
            queries1(0)
            query_transposes(0)
            with pe.Fori(0, B - 1) as b:
                batch1(b, True)
            batch1(B - 1, False)

            wr, wg1, wu1, wd1 = w1("router", KC), w1("gate", KC), w1("up", KC), w1("down", 1)
            wsg, wsu, wsd = w1("sgate", KC), w1("sup", KC), w1("sdown", 2)
            pe.wait_ge(s["a_upd"], B + 1)
            pe.wait_ge(s["lr_lo"], 3)

            def router_logits(c):
                pe.wait_ge(s["fx_lo"], NG * KC + c * KC + KC)
                for t in range(TG):
                    for k in range(KC):
                        last = product(pe, bR[:, t * E1:(t + 1) * E1], [gxT[:, j, k, t * P:(t + 1) * P] for j in range(2)],
                                       [wr[j][:, k, :] for j in range(2)], k == 0, k == KC - 1)
                last.then_inc(s["r_logit"], 1)

            def unit(c, u):
                pe.wait_ge(s["m_h"], c * U1 + u + 1)
                for ws, wb, bank, done in ((wsg, wg1, bS[u % 2], "m_g"), (wsu, wu1, [bPa, bPb][u % 2], "m_u")):
                    for k in range(KC):
                        tok = [gxT[:, j, k, :] for j in range(2)]
                        if u < 2:
                            last = product(pe, bank[:, :], [ws[j][:, k, u * P:(u + 1) * P] for j in range(2)], tok,
                                           k == 0, k == KC - 1)
                        else:
                            t, half = (u - 2) // 2, (u - 2) % 2
                            last = product(pe, bank[:, :], [a[:, t * P:(t + 1) * P] for a in tok],
                                           [wb[j][:, k, half * 512:(half + 1) * 512] for j in range(2)],
                                           k == 0, k == KC - 1)
                    last.then_inc(s[done], 1)

            def transpose_mixed(c):
                pe.wait_ge(s["m_mixed"], c + 1)
                for t in range(TG):
                    last = pe.transpose(bQ[:, t * P:(t + 1) * P], mixed[:, t, :], ident[:, :])
                last.then_inc(s["m_mT"], 1)

            def down_shared(c):
                pe.wait_ge(s["m_lo"], c * 2 + 2)
                pe.wait_ge(s["m_upd"], c * TG + 1)
                for t in range(TG):
                    y = [bV, bM][t // 2][:, (t % 2) * DM:(t % 2 + 1) * DM]
                    for f in range(2):
                        product(pe, y, [hT[:, f, j, t * P:(t + 1) * P] for j in range(2)], [wsd[j][:, f, :] for j in range(2)],
                                f == 0 and t % 2 == 0, False)

            def down_mixed(c):
                pe.wait_ge(s["m_mlo"], c + 1)
                for t in range(TG):
                    y = [bV, bM][t // 2][:, (t % 2) * DM:(t % 2 + 1) * DM]
                    last = product(pe, y, [mT[:, j, t * P:(t + 1) * P] for j in range(2)],
                                   [wd1[j][:, 0, :] for j in range(2)], False, True)
                    if t % 2:
                        last.then_inc(s["m_y"], 1)

            def front1(c, first):
                router_logits(c)
                if not first:
                    transpose_mixed(c - 1)
                unit(c, 0)
                unit(c, 1)
                if not first:
                    down_mixed(c - 1)
                unit(c, 2)
                unit(c, 3)
                down_shared(c)
                pe.wait_ge(s["r_w"], c + 1)
                for t in range(TG):
                    last = pe.transpose(bR[:, t * P:(t + 1) * P], chosen[:, t, :], ident[:, :])
                last.then_inc(s["r_wT"], 1)
                pe.wait_ge(s["r_wTc"], c + 1)
                for t in range(TG):
                    last = pe.matmul(bR[:, t * KB:(t + 1) * KB], WT[:, t * P:(t + 1) * P], mixp[:, :], start=True,
                                     stop=True, skip_group_check=True)
                last.then_inc(s["r_c"], 1)

            def group1(c, following):
                for u in range(4, U1):
                    unit(c, u)
                    if u == 7 and following:
                        transpose_tokens(c + 1, NG, TOKENS_1)
                if following:
                    front1(c + 1, False)

            transpose_tokens(0, NG, TOKENS_1)
            front1(0, True)
            with pe.Fori(0, NG - 1) as c:
                group1(c, True)
            group1(NG - 1, False)
            transpose_mixed(NG - 1)
            down_mixed(NG - 1)


def _rows(a, n):
    return a.reshape(n, 128, -1).transpose(1, 0, 2)


def _tables():
    inv = (np.float32(1.0) / np.float32(10000.0) ** (np.arange(0, D, 2, dtype=np.float32) / np.float32(D))).astype(np.float32)
    ang = np.outer(np.arange(L, dtype=np.float32), inv).astype(np.float32)
    ang = np.concatenate([ang, ang], -1)
    cos, sin = np.cos(ang).astype(np.float32), np.sin(ang).astype(np.float32)
    sin[:, :D // 2] *= -1
    return cos, sin


def kernel(**inputs):
    import concourse.bacc as _bacc
    import ml_dtypes
    from concourse.bass_utils import run_bass_kernel_spmd as _run

    a = {k: np.asarray(v) for k, v in inputs.items()}
    cos, sin = _tables()
    rot = np.concatenate([np.arange(D // 2, D), np.arange(0, D // 2)])
    qw, kw = a["L0_xattn_q_norm_w"], a["L0_xattn_k_norm_w"]
    f32 = np.float32
    arrays = {
        "x": _rows(a["x"].reshape(B * L, DM), B * NT),
        "ctxT": _rows(a["ctx_2048"].reshape(B * T, DM).T, KC),
        "gates": np.broadcast_to(np.concatenate([a["g_xattn"], a["g_ffn"]]), (P, 4)),
        "ident": np.eye(P, dtype=f32),
        "identb": np.eye(P).astype(ml_dtypes.bfloat16),
        "maskb": np.where(np.arange(P)[None, :] > np.arange(P)[:, None], MASKED, 0.0).astype(ml_dtypes.bfloat16),
        "cosT": cos.T, "sinT": sin.T,
        "cosR": _rows(cos, NT), "sinR": _rows(sin, NT),
        "qw": np.stack([qw, qw[rot]], 1),
        "kw": np.broadcast_to(np.stack([kw, kw[rot]]), (P, 2, D)),
        "w0_kv": np.stack([_rows(a["L0_xattn_" + n], KC) for n in ("wk_ctx", "wv_ctx", "wk", "wv")], 1).reshape(P, -1),
        "w0_q": _rows(a["L0_xattn_wq"], KC).reshape(P, -1),
        "w0_o": _rows(a["L0_xattn_wo"], H).reshape(P, -1),
        "w0_g": np.stack([_rows(w.T, KC) for w in a["L0_ffn_w_gate"]], 1).reshape(P, -1),
        "w0_u": np.stack([_rows(w.T, KC) for w in a["L0_ffn_w_up"]], 1).reshape(P, -1),
        "w0_d": np.stack([_rows(w.T, FC) for w in a["L0_ffn_w_down"]], 1).reshape(P, -1),
        "gw0": _rows(a["L0_ffn_gate_w"].T, KC),
        "w0_l1": np.concatenate([
            _rows(a[n].T if turned else a[n], k).reshape(P, -1)
            for n, k, turned in (("L1_xattn_wkv", KC, True), ("L1_ffn_w_router", KC, False), ("L1_ffn_w_gate", KC, False),
                                 ("L1_ffn_w_up", KC, False), ("L1_ffn_w_down", 1, False),
                                 ("L1_ffn_shared_w_gate", KC, False), ("L1_ffn_shared_w_up", KC, False),
                                 ("L1_ffn_shared_w_down", 2, False), ("L1_xattn_wq", KC, False),
                                 ("L1_xattn_wp", KC, False))], 1),
        "headmask": (np.arange(P)[:, None] // D1 == np.arange(HC)[None, :]).astype(f32),
        "keymask": (np.arange(P)[:, None] // T == np.arange(2)[None, :]).astype(f32),
        "rows1": np.broadcast_to(np.stack([a["L1_xattn_bq"], a["L1_xattn_bp"], a["L1_xattn_bkv"][DM:]]), (P, 3, DM)),
        "bk": a["L1_xattn_bkv"][:DM].reshape(KC, P).T,
        "iota": np.broadcast_to(np.arange(E1, dtype=f32), (P, E1)),
        "amp": a["L1_ffn_amplitudes"],
        "escale": a["L1_ffn_expert_scale"].reshape(P, 1),
    }
    arrays = {"in_" + k: np.ascontiguousarray(v) for k, v in arrays.items()}
    nc = _bacc.Bacc("TRN2", target_bir_lowering=False, num_devices=1)
    ap = {k[3:]: nc.dram_tensor(k, v.shape, mybir.dt.from_np(v.dtype), kind="ExternalInput").ap()
          for k, v in arrays.items()}
    out = nc.dram_tensor("out_0", (P, B * NT, DM), F32, kind="ExternalOutput").ap()
    flamingo_layers(nc, ap["x"], ap["ctxT"], ap["gates"], ap, {k: ap["w0_" + k] for k in ("kv", "q", "o", "g", "u", "d", "l1")}, out)
    r = _run(nc, [arrays], core_ids=[0])
    return np.ascontiguousarray(r.results[0]["out_0"].transpose(1, 0, 2)).reshape(B, L, DM)
```
